# Optimizing a Trainium2 kernel written in Bass

```python
import numpy as np
import jax
import jax.numpy as jnp

def _softmax(x, axis=-1):
    return jax.nn.softmax(x, axis=axis)

def _gelu(x):
    return jax.nn.gelu(x, approximate=True)

def _silu(x):
    return jax.nn.silu(x)

def _sigmoid(x):
    return jax.nn.sigmoid(x)

def _layernorm(x, axis=-1, eps=1e-05):
    m = jnp.mean(x, axis=axis, keepdims=True)
    v = jnp.var(x, axis=axis, keepdims=True)
    return (x - m) / jnp.sqrt(v + eps)

def _scatter_add(tgt, idx, src, axis=0):
    return tgt.at[idx].add(src)

def _segment_sum(src, seg, n):
    return jax.ops.segment_sum(src, seg, n)
kernel_name = 'mk_seq_preln_d1_jaxref_r4_15a2a5'

def setup_inputs(seed: int=0):
    np.random.seed(seed)
    _w = jnp.asarray

    def _L0_attn_setup():
        import jax, jax.numpy as jnp
        import numpy as np
        H, DK, DV, GG = (16, 128, 128, 16)
        NG = DK // GG
        SCALE = DK ** (-0.5)
        EPS = 1e-05

        def _short_conv(x, w):
            K = w.shape[1]
            xp = jnp.pad(x, ((0, 0), (K - 1, 0), (0, 0)))
            y = jax.lax.conv_general_dilated(xp, jnp.transpose(w)[:, None, :], (1,), 'VALID', dimension_numbers=('NWC', 'WIO', 'NWC'), feature_group_count=w.shape[0])
            return jax.nn.silu(y)

        def _l2norm(x, eps=1e-06):
            return x * jax.lax.rsqrt(jnp.sum(x * x, -1, keepdims=True) + eps)

        def _forward(hidden_states, Wq, Wk, Wv, conv_q, conv_k, conv_v, Wf1, Wf2, Wb, A_log, dt_bias, Wg, bg, norm_w, Wo):
            B, T, D = hidden_states.shape
            q = _short_conv(hidden_states @ Wq, conv_q).reshape(B, T, H, DK)
            k = _short_conv(hidden_states @ Wk, conv_k).reshape(B, T, H, DK)
            v = _short_conv(hidden_states @ Wv, conv_v).reshape(B, T, H, DV)
            q = _l2norm(q) * SCALE
            k = _l2norm(k)
            g_grouped = (hidden_states @ Wf1 @ Wf2).reshape(B, T, H, NG)
            g_eff = -jnp.exp(A_log)[:, None] * jax.nn.softplus(g_grouped + dt_bias.reshape(H, NG))
            g_eff = jnp.repeat(g_eff, GG, axis=-1)
            beta = jax.nn.sigmoid(hidden_states @ Wb)

            def step(S, inp):
                qt, kt, vt, gt, bt = inp
                S = S * jnp.exp(gt)[..., None]
                err = jnp.einsum('bhk,bhkv->bhv', kt, S)
                delta = bt[..., None] * (vt - err)
                S = S + kt[..., None] * delta[:, :, None, :]
                ot = jnp.einsum('bhk,bhkv->bhv', qt, S)
                return (S, ot)
            tm = lambda x: jnp.moveaxis(x, 1, 0)
            S0 = jnp.zeros((B, H, DK, DV), hidden_states.dtype)
            _, o = jax.lax.scan(step, S0, (tm(q), tm(k), tm(v), tm(g_eff), tm(beta)))
            o = jnp.moveaxis(o, 0, 1)
            gate = (hidden_states @ Wg + bg).reshape(B, T, H, DV)
            y = o * jax.nn.silu(gate)
            y = y * jax.lax.rsqrt(jnp.mean(y * y, -1, keepdims=True) + EPS) * norm_w
            return y.reshape(B, T, H * DV) @ Wo
        key = jax.random.key(seed)
        ks = jax.random.split(key, 16)
        B, T, D = (2, 256, 512)
        KD, VD = (H * DK, H * DV)
        init = lambda k, sh: jax.random.normal(k, sh, jnp.float32) * 0.02
        return {'hidden_states': jax.random.normal(ks[0], (B, T, D), jnp.float32), 'Wq': init(ks[1], (D, KD)), 'Wk': init(ks[2], (D, KD)), 'Wv': init(ks[3], (D, VD)), 'conv_q': init(ks[4], (KD, 4)), 'conv_k': init(ks[5], (KD, 4)), 'conv_v': init(ks[6], (VD, 4)), 'Wf1': init(ks[7], (D, DV)), 'Wf2': init(ks[8], (DV, H * NG)), 'Wb': init(ks[9], (D, H)), 'A_log': jnp.log(jax.random.uniform(ks[10], (H,), jnp.float32, 1.0, 16.0)), 'dt_bias': jnp.zeros((H * NG,), jnp.float32), 'Wg': init(ks[11], (D, VD)), 'bg': jnp.zeros((VD,), jnp.float32), 'norm_w': jnp.ones((DV,), jnp.float32), 'Wo': init(ks[12], (VD, D))}
    _L0_attn_in = _L0_attn_setup()

    def _L0_ffn_setup():
        import jax, jax.numpy as jnp
        import numpy as np
        D_MODEL = 512
        D_FF = 352
        N_EXPERTS = 6
        TOP_K = 2
        B, S = (8, 1024)
        key = jax.random.key(seed)
        ks = jax.random.split(key, 6)
        x = jax.random.normal(ks[0], (B, S, D_MODEL), dtype=jnp.float32)
        W1 = jax.random.normal(ks[1], (N_EXPERTS, D_MODEL, D_FF), dtype=jnp.float32) * 0.02
        b1 = jax.random.normal(ks[2], (N_EXPERTS, D_FF), dtype=jnp.float32) * 0.02
        W2 = jax.random.normal(ks[3], (N_EXPERTS, D_FF, D_MODEL), dtype=jnp.float32) * 0.02
        b2 = jax.random.normal(ks[4], (N_EXPERTS, D_MODEL), dtype=jnp.float32) * 0.02
        gate_W = jax.random.normal(ks[5], (N_EXPERTS, D_MODEL), dtype=jnp.float32) * 0.02
        return {'x': x, 'gate_W': gate_W, 'W1': W1, 'b1': b1, 'W2': W2, 'b2': b2}
    _L0_ffn_in = _L0_ffn_setup()
    _d = {'L0_attn_hidden_states': _L0_attn_in['hidden_states'], 'L0_attn_Wq': _L0_attn_in['Wq'], 'L0_attn_Wk': _L0_attn_in['Wk'], 'L0_attn_Wv': _L0_attn_in['Wv'], 'L0_attn_conv_q': _L0_attn_in['conv_q'], 'L0_attn_conv_k': _L0_attn_in['conv_k'], 'L0_attn_conv_v': _L0_attn_in['conv_v'], 'L0_attn_Wf1': _L0_attn_in['Wf1'], 'L0_attn_Wf2': _L0_attn_in['Wf2'], 'L0_attn_Wb': _L0_attn_in['Wb'], 'L0_attn_A_log': _L0_attn_in['A_log'], 'L0_attn_dt_bias': _L0_attn_in['dt_bias'], 'L0_attn_Wg': _L0_attn_in['Wg'], 'L0_attn_bg': _L0_attn_in['bg'], 'L0_attn_norm_w': _L0_attn_in['norm_w'], 'L0_attn_Wo': _L0_attn_in['Wo'], 'L0_ffn_gate_W': _L0_ffn_in['gate_W'], 'L0_ffn_W1': _L0_ffn_in['W1'], 'L0_ffn_b1': _L0_ffn_in['b1'], 'L0_ffn_W2': _L0_ffn_in['W2'], 'L0_ffn_b2': _L0_ffn_in['b2']}
    _x0 = _d['L0_attn_hidden_states']
    _d['L0_attn_hidden_states'] = jax.random.normal(jax.random.fold_in(jax.random.key(seed), 1), (4, 1024, 512), dtype=_x0.dtype)
    del _x0
    return _d

def reference(L0_attn_hidden_states, L0_attn_Wq, L0_attn_Wk, L0_attn_Wv, L0_attn_conv_q, L0_attn_conv_k, L0_attn_conv_v, L0_attn_Wf1, L0_attn_Wf2, L0_attn_Wb, L0_attn_A_log, L0_attn_dt_bias, L0_attn_Wg, L0_attn_bg, L0_attn_norm_w, L0_attn_Wo, L0_ffn_gate_W, L0_ffn_W1, L0_ffn_b1, L0_ffn_W2, L0_ffn_b2):

    def _L0_attn_ref(hidden_states, Wq, Wk, Wv, conv_q, conv_k, conv_v, Wf1, Wf2, Wb, A_log, dt_bias, Wg, bg, norm_w, Wo):
        import jax, jax.numpy as jnp
        import numpy as np
        H, DK, DV, GG = (16, 128, 128, 16)
        NG = DK // GG
        SCALE = DK ** (-0.5)
        EPS = 1e-05

        def _short_conv(x, w):
            K = w.shape[1]
            xp = jnp.pad(x, ((0, 0), (K - 1, 0), (0, 0)))
            y = jax.lax.conv_general_dilated(xp, jnp.transpose(w)[:, None, :], (1,), 'VALID', dimension_numbers=('NWC', 'WIO', 'NWC'), feature_group_count=w.shape[0])
            return jax.nn.silu(y)

        def _l2norm(x, eps=1e-06):
            return x * jax.lax.rsqrt(jnp.sum(x * x, -1, keepdims=True) + eps)

        def _forward(hidden_states, Wq, Wk, Wv, conv_q, conv_k, conv_v, Wf1, Wf2, Wb, A_log, dt_bias, Wg, bg, norm_w, Wo):
            B, T, D = hidden_states.shape
            q = _short_conv(hidden_states @ Wq, conv_q).reshape(B, T, H, DK)
            k = _short_conv(hidden_states @ Wk, conv_k).reshape(B, T, H, DK)
            v = _short_conv(hidden_states @ Wv, conv_v).reshape(B, T, H, DV)
            q = _l2norm(q) * SCALE
            k = _l2norm(k)
            g_grouped = (hidden_states @ Wf1 @ Wf2).reshape(B, T, H, NG)
            g_eff = -jnp.exp(A_log)[:, None] * jax.nn.softplus(g_grouped + dt_bias.reshape(H, NG))
            g_eff = jnp.repeat(g_eff, GG, axis=-1)
            beta = jax.nn.sigmoid(hidden_states @ Wb)

            def step(S, inp):
                qt, kt, vt, gt, bt = inp
                S = S * jnp.exp(gt)[..., None]
                err = jnp.einsum('bhk,bhkv->bhv', kt, S)
                delta = bt[..., None] * (vt - err)
                S = S + kt[..., None] * delta[:, :, None, :]
                ot = jnp.einsum('bhk,bhkv->bhv', qt, S)
                return (S, ot)
            tm = lambda x: jnp.moveaxis(x, 1, 0)
            S0 = jnp.zeros((B, H, DK, DV), hidden_states.dtype)
            _, o = jax.lax.scan(step, S0, (tm(q), tm(k), tm(v), tm(g_eff), tm(beta)))
            o = jnp.moveaxis(o, 0, 1)
            gate = (hidden_states @ Wg + bg).reshape(B, T, H, DV)
            y = o * jax.nn.silu(gate)
            y = y * jax.lax.rsqrt(jnp.mean(y * y, -1, keepdims=True) + EPS) * norm_w
            return y.reshape(B, T, H * DV) @ Wo
        return _forward(hidden_states, Wq, Wk, Wv, conv_q, conv_k, conv_v, Wf1, Wf2, Wb, A_log, dt_bias, Wg, bg, norm_w, Wo)

    def _L0_ffn_ref(x, gate_W, W1, b1, W2, b2):
        import jax, jax.numpy as jnp
        import numpy as np
        D_MODEL = 512
        D_FF = 352
        N_EXPERTS = 6
        TOP_K = 2
        B, S = (8, 1024)
        gate_logits = jnp.einsum('bd,ed->be', x.mean(axis=1), gate_W)
        gate_probs = jax.nn.softmax(gate_logits, axis=-1)
        topk_vals, topk_idx = jax.lax.top_k(gate_probs, TOP_K)
        topk_vals = topk_vals / topk_vals.sum(axis=-1, keepdims=True)
        W1g = W1[topk_idx]
        b1g = b1[topk_idx]
        W2g = W2[topk_idx]
        b2g = b2[topk_idx]
        h = jnp.einsum('bsd,bkdf->bksf', x, W1g) + b1g[:, :, None, :]
        h = jax.nn.gelu(h, approximate=False)
        eo = jnp.einsum('bksf,bkfd->bksd', h, W2g) + b2g[:, :, None, :]
        return jnp.einsum('bk,bksd->bsd', topk_vals, eo)
    x = L0_attn_hidden_states
    x = x + _L0_attn_ref(_layernorm(x, axis=-1), L0_attn_Wq, L0_attn_Wk, L0_attn_Wv, L0_attn_conv_q, L0_attn_conv_k, L0_attn_conv_v, L0_attn_Wf1, L0_attn_Wf2, L0_attn_Wb, L0_attn_A_log, L0_attn_dt_bias, L0_attn_Wg, L0_attn_bg, L0_attn_norm_w, L0_attn_Wo)
    x = x + _L0_ffn_ref(_layernorm(x, axis=-1), L0_ffn_gate_W, L0_ffn_W1, L0_ffn_b1, L0_ffn_W2, L0_ffn_b2)
    return x

_drawn_inputs = setup_inputs


def setup_inputs(seed=0):
    import zlib

    import numpy as np

    out = dict(_drawn_inputs(seed))
    spreads = {'L0_attn_dt_bias': (0.0, 0.8), 'L0_attn_bg': (0.0, 0.8), 'L0_attn_norm_w': (1.0, 0.6)}
    factors = {'L0_attn_Wq': 8.0,
     'L0_attn_Wk': 8.0,
     'L0_attn_Wv': 8.0,
     'L0_attn_conv_q': 8.0,
     'L0_attn_conv_k': 8.0,
     'L0_attn_conv_v': 8.0,
     'L0_attn_Wf1': 8.0,
     'L0_attn_Wf2': 8.0,
     'L0_attn_Wb': 8.0,
     'L0_attn_A_log': 8.0,
     'L0_attn_Wg': 8.0,
     'L0_attn_Wo': 8.0,
     'L0_ffn_b1': 64.0,
     'L0_ffn_b2': 28.308,
     'L0_ffn_gate_W': 4.872,
     'L0_ffn_W1': 6.223,
     'L0_ffn_W2': 5.695}
    for name, (base, spread) in spreads.items():
        noise = np.random.default_rng([zlib.crc32(name.encode()), seed]).standard_normal(out[name].shape)
        drawn = base * np.exp(spread * noise) if base else spread * noise
        out[name] = jnp.asarray(drawn.astype(out[name].dtype))
    for name, factor in factors.items():
        out[name] = (out[name] * factor).astype(out[name].dtype)
    return out
```

```python
from contextlib import ExitStack

import concourse.bass as bass
from concourse import mybir

P = 128
F32 = mybir.dt.float32
I32 = mybir.dt.int32
U32 = mybir.dt.uint32
ALU = mybir.AluOpType
ACT = mybir.ActivationFunctionType
AX_X = mybir.AxisListType.X


class Signal:

    def __init__(self, sem, per):
        self.sem, self.per = sem, per

    def at(self, unit, k):
        return unit * self.per + k


def wait_apart(eng, sem, value, passed):
    eng.wait_ge(sem, value)
    eng.sem_inc(passed, 1)


def preln_delta_moe(nc, x, Wq, Wk, Wv, conv_q, conv_k, conv_v, Wf1, Wf2, Wb, A_log, dt_bias, Wg, bg,
                    norm_w, Wo, gate_W, W1, b1, W2, b2, out):
    B, T, D = x.shape
    H = A_log.shape[0]
    HC = Wq.shape[1]
    NG = Wf2.shape[1] // H
    GG = P // NG
    KC = D // P
    J = T // P
    UC = B * P
    TAPS = conv_q.shape[1]
    HALO = TAPS - 1
    LEVELS = 7
    SCALE = float(P) ** -0.5
    L2_EPS, LN_EPS = 1e-6, 1e-5
    E, _, FF = W1.shape
    FCH = [(0, 128), (128, 128), (256, FF - 256)]
    NF = len(FCH)
    assert HC == H * P and UC == 512 and H * NG == P and H % 2 == 0 and J % 2 == 0 and 256 < FF <= 384
    TINY, GRAIN = 2.0 ** -80, 2.0 ** 46
    assert 1 << LEVELS == P

    y_scratch = nc.dram_tensor("y_scratch", [J, B, P, H, P], F32, kind="Internal").ap()
    beta_scratch = nc.dram_tensor("beta_scratch", [H, J, UC], F32, kind="Internal").ap()
    decay_scratch = nc.dram_tensor("decay_scratch", [H, NG, J, UC], F32, kind="Internal").ap()

    with ExitStack() as whole:
        bank = [whole.enter_context(nc.psum_tensor(f"bank{i}", [P, 512], F32)) for i in range(8)]
        ident = whole.enter_context(nc.sbuf_tensor("ident", [P, P], F32))
        ones = whole.enter_context(nc.sbuf_tensor("ones", [P, P], F32))
        ln_eps = whole.enter_context(nc.sbuf_tensor("ln_eps", [P, 1], F32))
        with ExitStack() as ctx:
            attention(nc, ctx, locals())
        with ExitStack() as ctx:
            mixture(nc, ctx, locals())


def attention(nc, ctx, env):
    (x, Wq, Wk, Wv, Wg, conv_q, conv_k, conv_v, Wf1, Wf2, Wb, A_log, dt_bias, bg, norm_w) = (env[n] for n in (
        "x", "Wq", "Wk", "Wv", "Wg", "conv_q", "conv_k", "conv_v", "Wf1", "Wf2", "Wb", "A_log", "dt_bias", "bg",
        "norm_w"))
    (B, T, D, H, NG, GG, KC, J, UC, TAPS, HALO, LEVELS, SCALE, L2_EPS, LN_EPS, TINY, GRAIN) = (env[n] for n in (
        "B", "T", "D", "H", "NG", "GG", "KC", "J", "UC", "TAPS", "HALO", "LEVELS", "SCALE", "L2_EPS", "LN_EPS", "TINY",
        "GRAIN"))
    y_scratch, beta_scratch, decay_scratch = env["y_scratch"], env["beta_scratch"], env["decay_scratch"]
    bank, ident, ones, ln_eps = env["bank"], env["ident"], env["ones"], env["ln_eps"]

    def sb(name, shape, dt=F32):
        return ctx.enter_context(nc.sbuf_tensor(name, shape, dt))

    def sem(name):
        return ctx.enter_context(nc.semaphore(name))

    def signal(name, per):
        return Signal(sem(name), per)

    xT = sb("xT", [P, KC, J * UC])
    mean_ones = sb("mean_ones", [P, P])
    level_mask = sb("level_mask", [P, LEVELS, UC // 2])
    pairs = sb("pairs", [P, LEVELS + 1, UC])
    state = sb("state", [P, UC])
    ident_less = sb("ident_less", [P, P])
    ZI = sb("ZI", [P, LEVELS - 1, UC])
    norm_w_col = sb("norm_w_col", [P, 1])
    l2_eps = sb("l2_eps", [P, 1])

    with ExitStack() as c0:
        def sb0(name, shape, dt=F32):
            return c0.enter_context(nc.sbuf_tensor(name, shape, dt))

        def sem0(name):
            return c0.enter_context(nc.semaphore(name))

        wf1 = sb0("wf1", [P, KC, P])
        wf2 = sb0("wf2", [P, P])
        wb = sb0("wb", [P, KC, H])
        dt_col = sb0("dt_col", [P, 1])
        alog_col = sb0("alog_col", [P, 1])
        rate_col = sb0("rate_col", [P, 1])
        xt = [sb0(f"xt{p}", [P, B, D]) for p in range(2)]
        stats = sb0("stats", [P, B, 6])
        mv = sb0("mv", [P, B, 2])
        log_var = sb0("log_var", [P, B])
        rstd = sb0("rstd", [P, B])
        f1_sb = sb0("f1_sb", [P, UC])
        b_exp = sb0("b_exp", [H, UC])
        b_den = sb0("b_den", [H, UC])
        b_out = sb0("b_out", [H, UC])
        z = sb0("z", [P, UC])
        z_abs = sb0("z_abs", [P, UC])
        z_exp = sb0("z_exp", [P, UC])
        z_s = sb0("z_s", [P, UC])
        z_s2 = sb0("z_s2", [P, UC])
        z_sum = sb0("z_sum", [P, UC])
        softplus = sb0("softplus", [P, UC])
        decay = sb0("decay", [P, UC])

        consts_loaded = sem0("consts_loaded")
        x_loaded = [sem0(f"x_loaded{p}") for p in range(2)]
        pool_steps = sem0("pool_steps")
        ln_steps = sem0("ln_steps")
        xn_ready = sem0("xn_ready")
        x_transposed = sem0("x_transposed")
        xT_ready = sem0("xT_ready")
        beta_logits_done = sem0("beta_logits_done")
        beta_exp_ready = sem0("beta_exp_ready")
        beta_steps = sem0("beta_steps")
        f1_done = sem0("f1_done")
        f1_ready = sem0("f1_ready")
        f2_done = sem0("f2_done")
        sp_act_steps = sem0("sp_act_steps")
        sp_vec_steps = sem0("sp_vec_steps")
        softplus_ready = sem0("softplus_ready")
        rate_steps = sem0("rate_steps")
        z_exp_ready = sem0("z_exp_ready")
        waits_passed0 = sem0("waits_passed0")
        decay_ready = sem0("decay_ready")
        scratch_stored = sem0("scratch_stored")
        NCONST = 5 + NG
        ATANH = [2.0 / n for n in range(1, 16, 2)]
        SP_STEPS = 4 + len(ATANH)

        block = c0.enter_context(nc.Block())

        @block.sync
        def _(sp):
            x_chunks = x.rearrange("b (j t) d -> j t b d", t=P)
            for p in range(2):
                sp.dma_start(xt[p][:], x_chunks[p]).then_inc(x_loaded[p], 16)
            sp.dma_start(wf1[:], Wf1.rearrange("(k p) f -> p k f", p=P)).then_inc(consts_loaded, 16)
            sp.dma_start(wf2[:], Wf2).then_inc(consts_loaded, 16)
            sp.dma_start(wb[:], Wb.rearrange("(k p) h -> p k h", p=P)).then_inc(consts_loaded, 16)
            sp.dma_start(dt_col[:], dt_bias.rearrange("(c o) -> c o", o=1)).then_inc(consts_loaded, 16)
            sp.dma_start(norm_w_col[:], norm_w.rearrange("(c o) -> c o", o=1)).then_inc(consts_loaded, 16)
            for g in range(NG):
                sp.dma_start(alog_col[g::NG, :], A_log.rearrange("(c o) -> c o", o=1)).then_inc(consts_loaded, 16)
            sp.sem_inc(scratch_stored, 32)

            def store(j):
                sp.wait_ge(beta_steps, j * 2 + 2)
                sp.dma_start(beta_scratch[:, bass.ds(j, 1), :].rearrange("h a c -> h (a c)"),
                             b_out[:]).then_inc(scratch_stored, 16)
                sp.wait_ge(decay_ready, j + 1)
                sp.dma_start(decay_scratch.rearrange("h g j c -> (h g) j c")[:, bass.ds(j, 1), :]
                             .rearrange("h a c -> h (a c)"), decay[:]).then_inc(scratch_stored, 16)

            with sp.Fori(0, J // 2 - 1) as jj:
                for p in range(2):
                    j = sp.snap(jj * 2 + p)
                    sp.wait_ge(x_transposed, j * KC + KC)
                    sp.dma_start(xt[p][:], x_chunks[bass.ds(j + 2, 1)].rearrange("a t b d -> (a t) b d")) \
                        .then_inc(x_loaded[p], 16)
                    store(j)
            for j in range(J - 2, J):
                store(j)
            sp.wait_ge(scratch_stored, 32 * (J + 1))

        @block.gpsimd
        def _(pool):
            nc.gpsimd.memset(ident[:], 0.0).then_inc(pool_steps, 1)
            pool.wait_ge(pool_steps, 1)
            nc.gpsimd.affine_select(out=ident[:], in_=ident[:], compare_op=ALU.not_equal, fill=1.0, base=0,
                                    pattern=[[-1, P]], channel_multiplier=1).then_inc(pool_steps, 1)
            nc.gpsimd.memset(ones[:], 1.0)
            nc.gpsimd.memset(mean_ones[:], 1.0 / P)
            nc.gpsimd.memset(ln_eps[:], LN_EPS)
            nc.gpsimd.memset(l2_eps[:], L2_EPS)
            nc.gpsimd.memset(level_mask[:], GRAIN).then_inc(pool_steps, 1)
            nc.gpsimd.memset(pairs[:], 0.0)
            nc.gpsimd.memset(state[:], 0.0)
            pool.wait_ge(pool_steps, 3)
            nc.gpsimd.tensor_scalar(ident_less[:], ident[:], -TINY, None, ALU.add)
            for l in range(LEVELS - 1):
                nc.gpsimd.tensor_copy(ZI[:, l].rearrange("p (b t) -> p b t", b=B),
                                      ident[:].unsqueeze(1).to_broadcast([P, B, P]))
            for l in range(LEVELS):
                half, blocks = 1 << l, P >> (l + 1)
                m = level_mask[:, l, :].rearrange("p (b m s) -> p b m s", b=B, m=blocks)
                nc.gpsimd.affine_select(out=m, in_=m, compare_op=ALU.is_ge, fill=0.0, base=0,
                                        pattern=[[0, B], [-2 * half, blocks], [0, half]],
                                        channel_multiplier=1).then_inc(pool_steps, 1)
                pool.wait_ge(pool_steps, 4 + 2 * l)
                nc.gpsimd.affine_select(out=m, in_=m, compare_op=ALU.is_ge, fill=0.0, base=half - 1,
                                        pattern=[[0, B], [2 * half, blocks], [0, half]],
                                        channel_multiplier=-1).then_inc(pool_steps, 1)

        @block.vector
        def _(dve):
            dve.wait_ge(rate_steps, 1)
            nc.vector.tensor_scalar(rate_col[:], alog_col[:], -1.0, None, ALU.mult).then_inc(rate_steps, 1)
            with dve.Fori(0, J // 2) as jj:
                for p in range(2):
                    j = dve.snap(jj * 2 + p)
                    dve.wait_ge(x_loaded[p], jj * 16 + 16)
                    for b in range(B):
                        last = nc.vector.bn_stats(stats[:, b, :], xt[p][:, b, :])
                    last.then_inc(ln_steps, 1)
                    wait_apart(dve, ln_steps, j * 4 + 1, waits_passed0)
                    for b in range(B):
                        last = nc.vector.bn_aggr(mv[:, b, :], stats[:, b, :])
                    last.then_inc(ln_steps, 1)
                    dve.wait_ge(ln_steps, j * 4 + 4)
                    for b in range(B):
                        last = nc.vector.tensor_scalar(xt[p][:, b, :], xt[p][:, b, :], mv[:, b, 0:1], rstd[:, b:b + 1],
                                                       ALU.subtract, ALU.mult)
                    last.then_inc(xn_ready, 1)
                    dve.wait_ge(beta_exp_ready, j + 1)
                    nc.vector.tensor_scalar(b_den[:], b_exp[:], 1.0, None, ALU.add).then_inc(beta_steps, 1)
                    dve.wait_ge(beta_steps, j * 2 + 1)
                    dve.wait_ge(scratch_stored, j * 32 + 32)
                    nc.vector.reciprocal(b_out[:], b_den[:]).then_inc(beta_steps, 1)
                    n = j * SP_STEPS

                    def chained(k, ins):
                        ins.then_inc(sp_vec_steps, 1)
                        dve.wait_ge(sp_vec_steps, n + k)

                    dve.wait_ge(z_exp_ready, j + 1)
                    chained(1, nc.vector.tensor_scalar(z_s[:], z_exp[:], 2.0, None, ALU.add))
                    chained(2, nc.vector.reciprocal(z_s[:], z_s[:]))
                    chained(3, nc.vector.tensor_tensor(z_s[:], z_s[:], z_exp[:], ALU.mult))
                    chained(4, nc.vector.tensor_tensor(z_s2[:], z_s[:], z_s[:], ALU.mult))
                    chained(5, nc.vector.tensor_scalar(z_sum[:], z_s2[:], ATANH[-1], None, ALU.mult))
                    for k, c in enumerate(ATANH[-2:0:-1]):
                        chained(6 + k, nc.vector.scalar_tensor_tensor(z_sum[:], z_sum[:], c, z_s2[:], ALU.add, ALU.mult))
                    chained(SP_STEPS, nc.vector.scalar_tensor_tensor(z_sum[:], z_sum[:], ATANH[0], z_s[:], ALU.add, ALU.mult))
                    nc.vector.scalar_tensor_tensor(softplus[:], z[:], 0.0, z_sum[:], ALU.max,
                                                   ALU.add).then_inc(softplus_ready, 1)

        @block.scalar
        def _(act):
            nc.scalar.preload_act_table_set("natural_log_exp_and_others")
            act.wait_ge(consts_loaded, 16 * NCONST)
            nc.scalar.activation(alog_col[:], alog_col[:], ACT.Exp).then_inc(rate_steps, 1)
            act.wait_ge(rate_steps, 2)
            act.wait_ge(pool_steps, 3)
            with act.Fori(0, J) as j:
                act.wait_ge(ln_steps, j * 4 + 2)
                nc.scalar.activation(log_var[:], mv[:, :, 1], ACT.Ln, bias=ln_eps[:, 0:1]).then_inc(ln_steps, 1)
                act.wait_ge(ln_steps, j * 4 + 3)
                nc.scalar.activation(rstd[:], log_var[:], ACT.Exp, scale=-0.5).then_inc(ln_steps, 1)
                for k in range(KC):
                    act.wait_ge(x_transposed, j * KC + (k + 1))
                    nc.scalar.activation(xT[:, k, bass.ds(j * UC, UC)], bank[k][:], ACT.Copy).then_inc(xT_ready, 1)
                act.wait_ge(beta_logits_done, j + 1)
                nc.scalar.activation(b_exp[:], bank[5][0:H, :], ACT.Exp, scale=-1.0).then_inc(beta_exp_ready, 1)
                act.wait_ge(f1_done, j + 1)
                nc.scalar.activation(f1_sb[:], bank[4][:], ACT.Copy).then_inc(f1_ready, 1)
                act.wait_ge(f2_done, j + 1)
                nc.scalar.activation(z[:], bank[6][:], ACT.Identity, bias=dt_col[:, 0:1]).then_inc(sp_act_steps, 1)
                act.wait_ge(sp_act_steps, j * 2 + 1)
                nc.scalar.activation(z_abs[:], z[:], ACT.Abs).then_inc(sp_act_steps, 1)
                act.wait_ge(sp_act_steps, j * 2 + 2)
                nc.scalar.activation(z_exp[:], z_abs[:], ACT.Exp, scale=-1.0).then_inc(z_exp_ready, 1)
                act.wait_ge(softplus_ready, j + 1)
                act.wait_ge(scratch_stored, j * 32 + 32)
                nc.scalar.activation(decay[:], softplus[:], ACT.Exp, scale=rate_col[:, 0:1]).then_inc(decay_ready, 1)

        @block.tensor
        def _(pe):
            pe.wait_ge(pool_steps, 2)
            pe.wait_ge(consts_loaded, 16 * NCONST)
            with pe.Fori(0, J // 2) as jj:
                for p in range(2):
                    j = pe.snap(jj * 2 + p)
                    pe.wait_ge(xn_ready, j + 1)
                    for k in range(KC):
                        for b in range(B):
                            last = nc.tensor.transpose(bank[k][:, b * P:(b + 1) * P], xt[p][:, b, k * P:(k + 1) * P],
                                                       ident[:])
                        last.then_inc(x_transposed, 1)
                    pe.wait_ge(xT_ready, j * KC + KC)
                    for k in range(KC):
                        last = nc.tensor.matmul(bank[5][0:H, :], wb[:, k, :], xT[:, k, bass.ds(j * UC, UC)],
                                                start=k == 0, stop=k == KC - 1)
                    last.then_inc(beta_logits_done, 1)
                    for k in range(KC):
                        last = nc.tensor.matmul(bank[4][:], wf1[:, k, :], xT[:, k, bass.ds(j * UC, UC)],
                                                start=k == 0, stop=k == KC - 1)
                    last.then_inc(f1_done, 1)
                    pe.wait_ge(f1_ready, j + 1)
                    nc.tensor.matmul(bank[6][:], wf2[:], f1_sb[:], start=True, stop=True).then_inc(f2_done, 1)

    weights = [sb(f"weights{p}", [P, 4, KC, P]) for p in range(2)]
    taps = [sb(f"taps{p}", [P, 3, TAPS]) for p in range(2)]
    bg_col = [sb(f"bg_col{p}", [P, 1]) for p in range(2)]
    pre = sb("pre", [P, 3, B, HALO + P])
    conv = sb("conv", [P, 3, B, P])
    silu = sb("silu", [P, 3, UC])
    v_u = sb("v_u", [P, UC])
    gate = sb("gate", [P, UC])
    squares = sb("squares", [P, 2, UC])
    log_sums = sb("log_sums", [P, 2, UC])
    rnorm = sb("rnorm", [P, 2, UC])
    decay_u = sb("decay_u", [P, UC])
    beta_u = sb("beta_u", [P, UC])
    k_hat = sb("k_hat", [P, UC])
    q_hat = sb("q_hat", [P, UC])
    KQ = sb("KQ", [P, 2, UC])
    KR = sb("KR", [P, UC])
    total = [decay_u] + [sb(f"total{l}", [P, UC >> l]) for l in range(1, LEVELS + 1)]
    X = sb("X", [P, UC])
    T_inv = sb("T_inv", [P, UC])
    k_rows = sb("k_rows", [P, UC])
    U_sb = sb("U_sb", [P, UC])
    delta = sb("delta", [P, UC])
    yg = sb("yg", [P, UC])
    y_sq = sb("y_sq", [P, UC])
    log_y = sb("log_y", [P, UC])
    y_rn = sb("y_rn", [P, UC])
    y_out = sb("y_out", [P, UC])

    HEAD_LOADS = 8
    dve_waits_passed, pool_waits_passed = sem("dve_waits_passed"), sem("pool_waits_passed")
    head_loaded = sem("head_loaded")
    unit_loaded = signal("unit_loaded", 32)
    y_stored = sem("y_stored")
    projected = signal("projected", 4)
    sums_done = signal("sums_done", 2)
    diag_done = signal("diag_done", 1)
    level_done = signal("level_done", LEVELS)
    z_done = signal("z_done", LEVELS - 1)
    x_done = signal("x_done", LEVELS - 1)
    t_done = signal("t_done", LEVELS - 1)
    k_transposed = signal("k_transposed", 1)
    u_done = signal("u_done", 1)
    o_state_done = signal("o_state_done", 1)
    delta_done = signal("delta_done", 1)
    o_done = signal("o_done", 1)
    s_done = signal("s_done", 1)
    y_sums_done = signal("y_sums_done", 1)
    halo_ready = signal("halo_ready", 1)
    conv_steps = signal("conv_steps", 3 * TAPS)
    hats_ready = signal("hats_ready", 1)
    unit_ready = signal("unit_ready", 1)
    scaled = signal("scaled", LEVELS)
    pairs_ready = signal("pairs_ready", LEVELS + 1)
    t1_ready = signal("t1_ready", 1)
    zi_ready = signal("zi_ready", LEVELS - 1)
    yg_ready = signal("yg_ready", 1)
    y_ready = signal("y_ready", 1)
    pre_ready = signal("pre_ready", 3)
    silu_ready = signal("silu_ready", 2)
    squares_ready = signal("squares_ready", 2)
    v_silu_ready = signal("v_silu_ready", 1)
    sums_taken = signal("sums_taken", 2)
    rnorm_ready = signal("rnorm_ready", 2)
    log_y_ready = signal("log_y_ready", 1)
    y_rn_ready = signal("y_rn_ready", 1)
    gate_ready = signal("gate_ready", 1)
    x_ready = signal("x_ready", LEVELS - 1)
    t_ready = signal("t_ready", LEVELS - 2)
    k_rows_ready = signal("k_rows_ready", 1)
    u_ready = signal("u_ready", 1)
    delta_ready = signal("delta_ready", 1)
    y_sq_ready = signal("y_sq_ready", 1)
    v_ready = signal("v_ready", 1)
    key_products = signal("key_products", LEVELS)
    keys_scaled = signal("keys_scaled", LEVELS)

    def wait(eng, sig, unit, k):
        eng.wait_ge(sig.sem, sig.at(unit, k))

    def cols(b):
        return slice(b * P, (b + 1) * P)

    def half_cols(b):
        return slice(b * (P // 2), (b + 1) * (P // 2))

    def halves(ap, l, which):
        if len(ap.shape) == 2:
            return ap.rearrange("p (m two s) -> p m two s", two=2, s=1 << l)[:, :, which, :]
        return ap.rearrange("p k (m two s) -> p k m two s", two=2, s=1 << l)[:, :, :, which, :]

    def by_batch(ap):
        return ap.rearrange("p (b t) -> p b t", b=B)

    def on_each_batch(ap):
        return ap.unsqueeze(1).to_broadcast([P, B, P])

    def walk(eng, step, first=None):
        step(0, None, 0, 0, None, False)

        def head(h, par, last):
            with eng.Fori(0, J - 1) as j:
                ub = eng.snap(h * J + j)
                step(par, par, ub + 1, j + 1, ub, False)
            ub = eng.snap(h * J + (J - 1)) if not isinstance(h, int) else h * J + J - 1
            if last:
                step(None, par, None, None, ub, True)
            else:
                step(1 - par, par, ub + 1, 0, ub, True)

        with eng.Fori(0, H // 2 - 1) as hp:
            for par in range(2):
                head(hp * 2 + par, par, False)
        head(H - 2, 0, False)
        head(H - 1, 1, True)

    block = ctx.enter_context(nc.Block())

    @block.sync
    def _(sp):
        def load_head(h, par):
            at = bass.ds(h * P, P)
            for m, W in enumerate((Wq, Wk, Wv, Wg)):
                sp.dma_start(weights[par][:, m, :, :], W.rearrange("(k p) n -> p k n", p=P)[:, :, at]) \
                    .then_inc(head_loaded, 16)
            for m, c in enumerate((conv_q, conv_k, conv_v)):
                sp.dma_start(taps[par][:, m, :], c[at, :]).then_inc(head_loaded, 16)
            sp.dma_start(bg_col[par][:], bg.rearrange("(c o) -> c o", o=1)[at, :]).then_inc(head_loaded, 16)

        def load_unit(h, j):
            sp.dma_start(beta_u[:], beta_scratch[bass.ds(h, 1), bass.ds(j, 1), :].rearrange("a b c -> (a b) c")
                         .to_broadcast([P, UC])).then_inc(unit_loaded.sem, 16)
            rows = decay_scratch[bass.ds(h, 1), :, bass.ds(j, 1), :].rearrange("a g b c -> (a g) (b c)")
            sp.dma_start(decay_u[:], rows.unsqueeze(1).to_broadcast([NG, GG, UC])).then_inc(unit_loaded.sem, 16)

        def store_y(h, j, ub):
            wait(sp, y_ready, ub, 1)
            sp.dma_start(y_scratch[bass.ds(j, 1), :, :, bass.ds(h, 1), :].rearrange("a b v h t -> v (a b h) t"),
                         by_batch(y_out[:])).then_inc(y_stored, 16)

        sp.sem_inc(y_stored, 16)
        load_head(0, 0)
        load_unit(0, 0)

        def head(h, par, last):
            with sp.Fori(0, J - 1) as j:
                ub = sp.snap(h * J + j)
                wait(sp, scaled, ub, 1)
                wait(sp, keys_scaled, ub, 1)
                load_unit(h, j + 1)
                store_y(h, j, ub)
            ub = sp.snap(h * J + (J - 1)) if not isinstance(h, int) else h * J + J - 1
            if not last:
                wait(sp, scaled, ub, 1)
                wait(sp, keys_scaled, ub, 1)
                load_unit(h + 1, 0)
            store_y(h, J - 1, ub)

        def load_next(h, par):
            wait(sp, gate_ready, h * J - 1, 1)
            load_head(h + 1, 1 - par)

        sp.wait_ge(head_loaded, 16 * HEAD_LOADS)
        load_head(1, 1)
        head(0, 0, False)
        with sp.Fori(0, H // 2 - 1) as hp:
            load_next(hp * 2 + 1, 1)
            head(hp * 2 + 1, 1, False)
            load_next(hp * 2 + 2, 0)
            head(hp * 2 + 2, 0, False)
        head(H - 1, 1, True)
        sp.wait_ge(y_stored, 16 * (H * J + 1))

    @block.tensor
    def _(pe):
        def step(par, par_b, ua, ja, ub, ends):
            def project(m, ks):
                if ua is None:
                    return
                if ks[0] == 0:
                    if m == 0:
                        if ub is None:
                            pe.wait_ge(head_loaded, 16 * HEAD_LOADS)
                        elif ends:
                            pe.wait_ge(head_loaded, (ub + 1 + J) * (16 * HEAD_LOADS // J))
                        if ub is not None:
                            wait(pe, pre_ready, ub, 3)
                    elif m == 1:
                        if ub is not None:
                            wait(pe, gate_ready, ub, 1)
                    else:
                        wait(pe, pre_ready, ua, m - 1)
                for k in ks:
                    last = nc.tensor.matmul(bank[m % 2][:], weights[par][:, m, k, :], xT[:, k, bass.ds(ja * UC, UC)],
                                            start=k == 0, stop=k == KC - 1)
                if ks[-1] == KC - 1:
                    last.then_inc(projected.sem, 1)

            def level(l):
                if l == 0:
                    wait(pe, unit_ready, ub, 1)
                else:
                    wait(pe, scaled, ub, l)
                    wait(pe, keys_scaled, ub, l)
                if l >= 1:
                    wait(pe, pairs_ready, ub, l)
                to = bank[3 + l % 2][:].rearrange("p (k b m s) -> p k b m s", k=2, b=B, s=1 << l)
                for b in range(B):
                    last = nc.tensor.matmul(to[:, :, b], KR[:, cols(b)], halves(KQ[:, :, cols(b)], l, 1),
                                            start=True, stop=True)
                last.then_inc(level_done.sem, 1)

            def inverse_z(l):
                wait(pe, pairs_ready, ub, l + 2)
                if l == 1:
                    wait(pe, t1_ready, ub, 1)
                else:
                    wait(pe, t_ready, ub, l - 1)
                for b in range(B):
                    last = nc.tensor.matmul(bank[5][:, half_cols(b)], pairs[:, l, cols(b)], halves(T_inv[:, cols(b)], l, 0),
                                            start=True, stop=True)
                last.then_inc(z_done.sem, 1)

            def inverse_xt(l):
                wait(pe, zi_ready, ub, l)
                if l >= 2:
                    wait(pe, x_ready, ub, l - 1)
                if l < LEVELS - 1:
                    for b in range(B):
                        last = nc.tensor.matmul(bank[7][:, half_cols(b)], X[:, cols(b)], halves(ZI[:, l - 1, cols(b)], l, 0),
                                                start=True, stop=True)
                    last.then_inc(t_done.sem, 1)
                for b in range(B):
                    last = nc.tensor.matmul(bank[6][:, half_cols(b)], ZI[:, l - 1, cols(b)], halves(X[:, cols(b)], l, 1),
                                            start=True, stop=True)
                last.then_inc(x_done.sem, 1)

            def sums(m):
                if ua is None:
                    return
                wait(pe, squares_ready, ua, m + 1)
                if m == 1:
                    wait(pe, sums_taken, ua, 1)
                nc.tensor.matmul(bank[2][:], ones[:], squares[:, m, :], start=True, stop=True).then_inc(sums_done.sem, 1)

            if ub is None:
                for m in range(4):
                    project(m, range(KC))
                sums(0)
                sums(1)
                return

            wait(pe, unit_ready, ub, 1)
            for b in range(B):
                last = nc.tensor.matmul(bank[4][:, cols(b)], KR[:, cols(b)], q_hat[:, cols(b)], start=True, stop=True)
            last.then_inc(diag_done.sem, 1)
            level(0)
            project(0, (0, 1))
            level(1)
            wait(pe, pairs_ready, ub, 2)
            for b in range(B):
                last = nc.tensor.transpose(bank[7][:, cols(b)], pairs[:, 0, cols(b)], ident[:])
            last.then_inc(t_done.sem, 1)
            project(0, (2, 3))
            level(2)
            inverse_z(1)
            project(1, (0,))
            inverse_xt(1)
            project(1, (1,))
            level(3)
            inverse_z(2)
            project(1, (2,))
            inverse_xt(2)
            project(1, (3,))
            level(4)
            inverse_z(3)
            project(2, (0, 1))
            inverse_xt(3)
            project(2, (2,))
            level(5)
            inverse_z(4)
            project(2, (3,))
            inverse_xt(4)
            sums(0)
            level(6)
            inverse_z(5)
            project(3, (0,))
            inverse_xt(5)
            sums(1)
            wait(pe, keys_scaled, ub, LEVELS)
            wait(pe, scaled, ub, LEVELS)
            wait(pe, pairs_ready, ub, LEVELS)
            for b in range(B):
                last = nc.tensor.transpose(bank[4][:, cols(b)], KR[:, cols(b)], ident[:])
            last.then_inc(k_transposed.sem, 1)
            inverse_z(6)
            wait(pe, pairs_ready, ub, LEVELS + 1)
            wait(pe, v_ready, ub, 1)
            for b in range(B):
                nc.tensor.matmul(bank[3][:, cols(b)], v_u[:, cols(b)], ident[:], start=True, stop=False)
                last = nc.tensor.matmul(bank[3][:, cols(b)], KQ[:, 0, cols(b)], state[:, cols(b)], start=False, stop=True)
            last.then_inc(u_done.sem, 1)
            project(3, (1, 2))
            inverse_xt(6)
            wait(pe, x_ready, ub, LEVELS - 1)
            for b in range(B):
                last = nc.tensor.matmul(bank[6][:, cols(b)], state[:, cols(b)], KQ[:, 1, cols(b)], start=b == 0,
                                        stop=False, skip_group_check=True)
            last.then_inc(o_state_done.sem, 1)
            project(3, (3,))
            wait(pe, u_ready, ub, 1)
            for b in range(B):
                last = nc.tensor.matmul(bank[5][:, cols(b)], X[:, cols(b)], U_sb[:, cols(b)], start=True, stop=True)
            last.then_inc(delta_done.sem, 1)
            wait(pe, delta_ready, ub, 1)
            for b in range(B):
                last = nc.tensor.matmul(bank[6][:, cols(b)], delta[:, cols(b)], pairs[:, LEVELS, cols(b)], start=False,
                                        stop=b == B - 1, skip_group_check=True)
            last.then_inc(o_done.sem, 1)
            wait(pe, k_rows_ready, ub, 1)
            for b in range(B):
                last = nc.tensor.matmul(bank[7][:, cols(b)], k_rows[:, cols(b)], delta[:, cols(b)], start=True, stop=True)
            last.then_inc(s_done.sem, 1)
            if ua is not None:
                wait(pe, sums_taken, ua, 2)
            wait(pe, y_sq_ready, ub, 1)
            nc.tensor.matmul(bank[2][:], mean_ones[:], y_sq[:], start=True, stop=True).then_inc(y_sums_done.sem, 1)

        walk(pe, step)

    @block.vector
    def _(dve):
        def step(par, par_b, ua, ja, ub, ends):
            def convolve(m):
                if ua is None:
                    return
                wait(dve, pre_ready, ua, m + 1)
                if ub is not None:
                    if m < 2:
                        wait(dve, silu_ready, ub, m + 1)
                    else:
                        wait(dve, v_silu_ready, ub, 1)
                nc.vector.tensor_scalar(conv[:, m], pre[:, m, :, 0:P], taps[par][:, m, 0:1], None,
                                        ALU.mult).then_inc(conv_steps.sem, 1)
                for t in range(1, TAPS):
                    wait(dve, conv_steps, ua, m * TAPS + t)
                    nc.vector.scalar_tensor_tensor(conv[:, m], pre[:, m, :, t:t + P], taps[par][:, m, t:t + 1], conv[:, m],
                                                   ALU.mult, ALU.add).then_inc(conv_steps.sem, 1)

            def scale(l):
                wait(dve, level_done, ub, l + 1)
                if l == 0:
                    wait(dve, unit_ready, ub, 1)
                else:
                    wait(dve, scaled, ub, l)
                blocks = UC >> (l + 1)
                pair = total[l][:].rearrange("p (m two) -> p m two", two=2)
                first = pair[:, :, 0:1]
                second_halves = halves(KQ[:], l, 1)
                nc.vector.tensor_tensor(second_halves, second_halves,
                                        first.unsqueeze(1).to_broadcast([P, 2, blocks, 1 << l]), ALU.mult)
                nc.vector.tensor_tensor(total[l + 1][:], pair[:, :, 0], pair[:, :, 1], ALU.mult).then_inc(scaled.sem, 1)

            def keep_pairs(l):
                blocks = UC >> (l + 1)
                src = bank[3 + l % 2][:].rearrange("p (k m s) -> p k m s", k=2, s=1 << l)
                wait_apart(dve, pairs_ready.sem, pairs_ready.at(ub, l + 1), dve_waits_passed)
                mask = level_mask[:, l].rearrange("p (m s) -> p m s", s=1 << l)
                nc.vector.copy_predicated(halves(pairs[:, LEVELS], l, 1), mask.bitcast(I32), src[:, 1])
                nc.vector.scalar_tensor_tensor(halves(pairs[:, l], l, 1), src[:, 0], 1.0 / GRAIN, mask, ALU.mult,
                                               ALU.mult).then_inc(pairs_ready.sem, 1)

            def add_identity_to_z(l):
                wait(dve, z_done, ub, l)
                blocks = P >> (l + 1)
                for b in range(B):
                    last = nc.vector.scalar_tensor_tensor(
                        halves(ZI[:, l - 1, cols(b)], l, 0),
                        bank[5][:, half_cols(b)].rearrange("p (m s) -> p m s", m=blocks), TINY,
                        halves(ident_less[:], l, 0), ALU.add, ALU.add)
                last.then_inc(zi_ready.sem, 1)

            def take_x(l):
                wait(dve, x_done, ub, l)
                nc.vector.tensor_scalar(halves(X[:], l, 1), bank[6][:, 0:UC // 2].rearrange("p (m s) -> p m s", s=1 << l),
                                        TINY, -TINY, ALU.add, ALU.add).then_inc(x_ready.sem, 1)

            def unit_inputs():
                if ua is None:
                    return
                wait(dve, rnorm_ready, ua, 2)
                wait(dve, unit_loaded, ua, 32)
                nc.vector.tensor_tensor(k_hat[:], silu[:, 1], rnorm[:, 1], ALU.mult)
                nc.vector.scalar_tensor_tensor(q_hat[:], silu[:, 0], SCALE, rnorm[:, 0], ALU.mult,
                                               ALU.mult).then_inc(hats_ready.sem, 1)
                wait(dve, hats_ready, ua, 1)
                if ub is not None:
                    wait(dve, k_transposed, ub, 1)
                nc.vector.tensor_tensor(KR[:], k_hat[:], beta_u[:], ALU.mult)
                if ub is not None:
                    wait(dve, u_done, ub, 1)
                nc.vector.scalar_tensor_tensor(KQ[:, 0], k_hat[:], -1.0, decay_u[:], ALU.mult, ALU.mult)
                if ub is not None:
                    wait(dve, o_state_done, ub, 1)
                nc.vector.tensor_tensor(KQ[:, 1], q_hat[:], decay_u[:], ALU.mult).then_inc(unit_ready.sem, 1)

            if ua is not None:
                if ub is None or ends:
                    if ub is not None:
                        wait(dve, conv_steps, ub, 3 * TAPS)
                    nc.vector.memset(pre[:, :, :, 0:HALO], 0.0).then_inc(halo_ready.sem, 1)
                else:
                    wait(dve, conv_steps, ub, 3 * TAPS)
                    nc.vector.tensor_copy(pre[:, :, :, 0:HALO], pre[:, :, :, P:P + HALO]).then_inc(halo_ready.sem, 1)
            if ub is None:
                for m in range(3):
                    convolve(m)
                unit_inputs()
                return

            wait_apart(dve, diag_done.sem, diag_done.at(ub, 1), dve_waits_passed)
            nc.vector.copy_predicated(by_batch(pairs[:, LEVELS]), on_each_batch(ident[:].bitcast(I32)),
                                      by_batch(bank[4][:])).then_inc(pairs_ready.sem, 1)
            for l in range(LEVELS):
                scale(l)
                keep_pairs(l)
                if l == 0:
                    wait(dve, pairs_ready, ub, 2)
                    nc.vector.tensor_tensor(by_batch(X[:]), by_batch(pairs[:, 0]), on_each_batch(ident[:]), ALU.add)
                if l == 1:
                    wait(dve, t_done, ub, 1)
                    nc.vector.tensor_tensor(by_batch(T_inv[:]), by_batch(bank[7][:]), on_each_batch(ident[:]),
                                            ALU.add).then_inc(t1_ready.sem, 1)
                if l >= 3:
                    take_x(l - 2)
                if l >= 2:
                    add_identity_to_z(l - 1)
                if l == 2:
                    convolve(0)
                if l == 4:
                    convolve(1)
                if l == 5:
                    convolve(2)
            take_x(LEVELS - 2)
            add_identity_to_z(LEVELS - 1)
            take_x(LEVELS - 1)
            unit_inputs()
            wait(dve, o_done, ub, 1)
            wait(dve, gate_ready, ub, 1)
            nc.vector.tensor_tensor(yg[:], bank[6][:], gate[:], ALU.mult).then_inc(yg_ready.sem, 1)
            wait(dve, s_done, ub, 1)
            if ends:
                nc.vector.memset(state[:], 0.0)
            else:
                for b in range(B):
                    nc.vector.scalar_tensor_tensor(state[:, cols(b)], state[:, cols(b)], total[LEVELS][:, b:b + 1],
                                                   bank[7][:, cols(b)], ALU.mult, ALU.add)
            wait(dve, y_rn_ready, ub, 1)
            dve.wait_ge(y_stored, ub * 16 + 16)
            nc.vector.scalar_tensor_tensor(y_out[:], yg[:], norm_w_col[:, 0:1], y_rn[:], ALU.mult,
                                           ALU.mult).then_inc(y_ready.sem, 1)

        walk(dve, step)

    @block.scalar
    def _(act):
        def step(par, par_b, ua, ja, ub, ends):
            def take_projection(m):
                if ua is None:
                    return
                wait(act, projected, ua, m + 1)
                if m == 0:
                    wait(act, halo_ready, ua, 1)
                nc.scalar.activation(pre[:, m, :, HALO:HALO + P], by_batch(bank[m % 2][:]),
                                     ACT.Copy).then_inc(pre_ready.sem, 1)

            def silu_squares(m):
                if ua is None:
                    return
                wait(act, conv_steps, ua, (m + 1) * TAPS)
                if m == 0 and ub is not None:
                    wait(act, unit_ready, ub, 1)
                nc.scalar.activation(silu[:, m], conv[:, m].rearrange("p b t -> p (b t)"),
                                     ACT.Silu).then_inc(silu_ready.sem, 1)
                wait(act, silu_ready, ua, m + 1)
                nc.scalar.activation(squares[:, m], silu[:, m], ACT.Square).then_inc(squares_ready.sem, 1)

            def silu_v():
                if ua is None:
                    return
                wait(act, conv_steps, ua, 3 * TAPS)
                if ub is not None:
                    wait(act, v_ready, ub, 1)
                nc.scalar.activation(silu[:, 2], conv[:, 2].rearrange("p b t -> p (b t)"),
                                     ACT.Silu).then_inc(v_silu_ready.sem, 1)

            def silu_gate():
                wait(act, projected, ub, 4)
                nc.scalar.activation(gate[:], bank[1][:], ACT.Silu, bias=bg_col[par_b][:, 0:1]).then_inc(gate_ready.sem, 1)

            def inverse_norm(m):
                if ua is None:
                    return
                wait(act, sums_done, ua, m + 1)
                if m == 0 and ub is not None:
                    wait(act, unit_ready, ub, 1)
                nc.scalar.activation(log_sums[:, m], bank[2][:], ACT.Ln, bias=l2_eps[:, 0:1]).then_inc(sums_taken.sem, 1)
                wait(act, sums_taken, ua, m + 1)
                nc.scalar.activation(rnorm[:, m], log_sums[:, m], ACT.Exp, scale=-0.5).then_inc(rnorm_ready.sem, 1)

            def take_t(l):
                wait(act, t_done, ub, l + 1)
                nc.scalar.activation(halves(T_inv[:], l, 0), bank[7][:, 0:UC // 2].rearrange("p (m s) -> p m s", s=1 << l),
                                     ACT.Copy).then_inc(t_ready.sem, 1)

            if ub is None:
                for m in range(3):
                    take_projection(m)
                silu_squares(0)
                silu_squares(1)
                silu_v()
                nc.scalar.preload_act_table_set("natural_log_exp_and_others")
                inverse_norm(0)
                inverse_norm(1)
                return

            take_projection(0)
            silu_gate()
            take_t(1)
            silu_squares(0)
            take_t(2)
            take_projection(1)
            take_t(3)
            take_projection(2)
            silu_squares(1)
            take_t(4)
            silu_v()
            nc.scalar.preload_act_table_set("natural_log_exp_and_others")
            inverse_norm(0)
            take_t(5)
            inverse_norm(1)
            wait(act, k_transposed, ub, 1)
            nc.scalar.activation(k_rows[:], bank[4][:], ACT.Copy).then_inc(k_rows_ready.sem, 1)
            wait(act, u_done, ub, 1)
            nc.scalar.activation(U_sb[:], bank[3][:], ACT.Copy).then_inc(u_ready.sem, 1)
            wait(act, delta_done, ub, 1)
            nc.scalar.activation(delta[:], bank[5][:], ACT.Copy).then_inc(delta_ready.sem, 1)
            wait(act, yg_ready, ub, 1)
            nc.scalar.activation(y_sq[:], yg[:], ACT.Square).then_inc(y_sq_ready.sem, 1)
            wait(act, y_sums_done, ub, 1)
            nc.scalar.activation(log_y[:], bank[2][:], ACT.Ln, bias=ln_eps[:, 0:1]).then_inc(log_y_ready.sem, 1)
            wait(act, log_y_ready, ub, 1)
            nc.scalar.activation(y_rn[:], log_y[:], ACT.Exp, scale=-0.5).then_inc(y_rn_ready.sem, 1)

        walk(act, step)

    @block.gpsimd
    def _(pool):
        def scale_keys(ub, l):
            if l == 0:
                wait_apart(pool, unit_ready.sem, unit_ready.at(ub, 1), pool_waits_passed)
            else:
                wait_apart(pool, scaled.sem, scaled.at(ub, l), pool_waits_passed)
                wait_apart(pool, keys_scaled.sem, keys_scaled.at(ub, l), pool_waits_passed)
            wait_apart(pool, level_done.sem, level_done.at(ub, l + 1), pool_waits_passed)
            first_halves = halves(KR[:], l, 0)
            second = total[l][:].rearrange("p (m two) -> p m two", two=2)[:, :, 1:2]
            nc.gpsimd.tensor_tensor(first_halves, first_halves, second.to_broadcast([P, UC >> (l + 1), 1 << l]),
                                    ALU.mult).then_inc(key_products.sem, 1)
            wait_apart(pool, key_products.sem, key_products.at(ub, l + 1), pool_waits_passed)
            nc.gpsimd.tensor_scalar(first_halves, first_halves, TINY, -TINY, ALU.add,
                                    ALU.add).then_inc(keys_scaled.sem, 1)

        def step(par, par_b, ua, ja, ub, ends):
            if ub is not None:
                for l in range(LEVELS):
                    scale_keys(ub, l)
            if ua is not None:
                wait_apart(pool, v_silu_ready.sem, v_silu_ready.at(ua, 1), pool_waits_passed)
                if ub is not None:
                    wait_apart(pool, u_done.sem, u_done.at(ub, 1), pool_waits_passed)
                nc.gpsimd.tensor_copy(v_u[:], silu[:, 2]).then_inc(v_ready.sem, 1)

        walk(pool, step)

def mixture(nc, ctx, env):
    (x, Wo, gate_W, W1, b1, W2, b2, out, y_scratch, bank, ident, ones, ln_eps) = (env[n] for n in (
        "x", "Wo", "gate_W", "W1", "b1", "W2", "b2", "out", "y_scratch", "bank", "ident", "ones", "ln_eps"))
    (B, T, D, H, KC, J, E, FF, FCH, NF, LN_EPS) = (env[n] for n in (
        "B", "T", "D", "H", "KC", "J", "E", "FF", "FCH", "NF", "LN_EPS"))
    TOP = 2
    HALF_T = T // 2
    HALVES = T // 512
    GROUPS = HALVES * TOP * NF
    LAST = FCH[-1][1]

    def sb(name, shape, dt=F32):
        return ctx.enter_context(nc.sbuf_tensor(name, shape, dt))

    def sem(name):
        return ctx.enter_context(nc.semaphore(name))

    wo = sb("wo", [P, H, D])
    gate_w = sb("gate_w", [P, KC, E])
    y_in = [sb(f"y_in{p}", [P, H, P]) for p in range(2)]
    x_in = [sb(f"x_in{p}", [P, D]) for p in range(2)]
    x1 = sb("x1", [P, J, D])
    xn = [sb(f"xn{p}", [P, D]) for p in range(2)]
    xnT = sb("xnT", [P, KC, T])
    stats = sb("stats2", [P, 6])
    mv = sb("mv2", [P, 2])
    log_var = sb("log_var2", [P, 1])
    rstd = sb("rstd2", [P, 1])
    token_sum = sb("token_sum", [P, KC])
    logits = sb("logits", [1, 8])
    top_val = sb("top_val", [1, 8])
    top_idx = sb("top_idx", [1, 8], U32)
    neg_max = sb("neg_max", [1, 1])
    exps = sb("exps", [1, E])
    exp_sum = sb("exp_sum", [1, 1])
    top_exp = sb("top_exp", [1, TOP])
    inv_sum = sb("inv_sum", [1, 1])
    top_prob = sb("top_prob", [1, TOP])
    prob_sum = sb("prob_sum", [1, 1])
    inv_prob = sb("inv_prob", [1, 1])
    share = sb("share", [1, TOP])
    share_all = sb("share_all", [P, TOP])
    w1 = sb("w1", [P, TOP, KC, FF])
    b1_col = sb("b1_col", [P, TOP, NF])
    w2 = sb("w2", [P, TOP, NF, D])
    w2_share = sb("w2_share", [P, TOP, NF, D])
    b2_row = sb("b2_row", [1, TOP, D])
    b2_part = sb("b2_part", [1, D])
    b2_mix = sb("b2_mix", [1, D])
    hT = sb("hT", [P, TOP, NF, T])
    o_out = [sb(f"o_out{p}", [P, D]) for p in range(2)]

    consts_loaded = sem("consts_loaded2")
    tile_loaded = [sem(f"tile_loaded{p}") for p in range(2)]
    experts_loaded = sem("experts_loaded")
    out_stored = [sem(f"out_stored{p}") for p in range(2)]
    attn_done = sem("attn_done")
    x1_ready = sem("x1_ready")
    ln_steps = sem("ln_steps2")
    xn_ready = sem("xn_ready2")
    xn_transposed = sem("xn_transposed")
    xnT_ready = sem("xnT_ready")
    token_sum_ready = sem("token_sum_ready")
    logits_done = sem("logits_done")
    route_steps = sem("route_steps")
    pads_ready = sem("pads_ready")
    dve_waits_passed, sp_waits_passed = sem("dve_waits_passed2"), sem("sp_waits_passed")
    choice_ready = sem("choice_ready")
    exps_ready = sem("exps_ready")
    share_ready = sem("share_ready")
    share_spread = sem("share_spread")
    mix_steps = sem("mix_steps")
    w2_ready = sem("w2_ready")
    h_done = sem("h_done")
    h_ready = sem("h_ready")
    ffn_done = sem("ffn_done")
    o_ready = sem("o_ready")
    EXPERT_LOADS = 16 * TOP * 6
    ROUTE_STEPS = 7

    block = ctx.enter_context(nc.Block())

    @block.sync
    def _(sp):
        sp.dma_start(wo[:], Wo.rearrange("(h v) d -> v h d", v=P)).then_inc(consts_loaded, 16)
        for k in range(KC):
            sp.dma_start(gate_w[:, k, :], gate_W.rearrange("e (k p) -> p k e", p=P)[:, k, :],
                         allow_slow_non_contiguous=True).then_inc(consts_loaded, 16)
        with sp.Fori(0, B) as b:
            for j in range(J):
                sp.wait_ge(x1_ready, b * J + (j + 1))
                sp.dma_start(y_in[j % 2][:], y_scratch[j, bass.ds(b, 1)].rearrange("a v h t -> (a v) h t")) \
                    .then_inc(tile_loaded[j % 2], 16)
                sp.dma_start(x_in[j % 2][:], x[bass.ds(b, 1), j * P:(j + 1) * P, :].rearrange("a t d -> (a t) d")) \
                    .then_inc(tile_loaded[j % 2], 16)
            wait_apart(sp, choice_ready, b + 1, sp_waits_passed)
            for n in range(TOP):
                e = sp.value_load(top_idx[0:1, n:n + 1], min_val=0, max_val=E - 1)
                at = bass.ds(e, 1)
                sp.dma_start(w1[:, n], W1[at].rearrange("a (k p) f -> p (a k) f", p=P)).then_inc(experts_loaded, 16)
                sp.dma_start(b1_col[:, n, 0:2], b1[at, 0:256].rearrange("a (c p) -> p (a c)", p=P),
                             allow_slow_non_contiguous=True).then_inc(experts_loaded, 16)
                sp.dma_start(b1_col[0:LAST, n, 2:3], b1[at, 256:FF].rearrange("a p -> p a"),
                             allow_slow_non_contiguous=True).then_inc(experts_loaded, 16)
                sp.dma_start(w2[:, n, 0:2], W2[at, 0:256, :].rearrange("a (c p) d -> p (a c) d", p=P)).then_inc(experts_loaded, 16)
                sp.dma_start(w2[0:LAST, n, 2], W2[at, 256:FF, :].rearrange("a p d -> (a p) d")).then_inc(experts_loaded, 16)
                sp.dma_start(b2_row[:, n], b2[at, :]).then_inc(experts_loaded, 16)

    @block.tensor
    def _(pe):
        def transpose_tile(b, j):
            pe.wait_ge(xn_ready, b * J + (j + 1))
            if j >= 2:
                pe.wait_ge(xnT_ready, b * J + (j - 1))
            for k in range(KC):
                last = nc.tensor.transpose(bank[2 + j % 2][:, k * P:(k + 1) * P], xn[j % 2][:, k * P:(k + 1) * P], ident[:])
            last.then_inc(xn_transposed, 1)

        pe.wait_ge(consts_loaded, 16 * (1 + KC))
        with pe.Fori(0, B) as b:
            for j in range(J):
                pe.wait_ge(tile_loaded[j % 2], b * (16 * J) + 32 * (j // 2 + 1))
                for h in range(H):
                    last = nc.tensor.matmul(bank[j % 2][:], y_in[j % 2][:, h, :], wo[:, h, :], start=h == 0, stop=h == H - 1)
                last.then_inc(attn_done, 1)
                if j >= 1:
                    transpose_tile(b, j - 1)
            transpose_tile(b, J - 1)
            pe.wait_ge(token_sum_ready, b + 1)
            for k in range(KC):
                last = nc.tensor.matmul(bank[2][0:1, 0:E], token_sum[:, k:k + 1], gate_w[:, k, :], start=k == 0, stop=k == KC - 1)
            last.then_inc(logits_done, 1)
            pe.wait_ge(share_ready, b + 1)
            nc.tensor.matmul(bank[3][:, 0:TOP], ones[0:1, :], share[:], start=True, stop=True).then_inc(share_spread, 1)
            pe.wait_ge(experts_loaded, b * EXPERT_LOADS + EXPERT_LOADS)
            g = 0
            for t in range(HALVES):
                for n in range(TOP):
                    for c, (f0, fn) in enumerate(FCH):
                        if g >= 2:
                            pe.wait_ge(h_ready, b * GROUPS + (g - 1))
                        for k in range(KC):
                            last = nc.tensor.matmul(bank[4 + g % 2][0:fn, :], w1[:, n, k, f0:f0 + fn],
                                                    xnT[:, k, t * 512:(t + 1) * 512], start=k == 0, stop=k == KC - 1)
                        last.then_inc(h_done, 1)
                        g += 1
            pe.wait_ge(w2_ready, b + 1)
            pe.wait_ge(h_ready, b * GROUPS + GROUPS)
            for j in range(J):
                if j >= 2:
                    pe.wait_ge(o_ready, b * J + (j - 1))
                to = bank[6 + j % 2]
                nc.tensor.matmul(to[:], ones[0:1, :], b2_mix[:], start=True, stop=False)
                for n in range(TOP):
                    for c, (f0, fn) in enumerate(FCH):
                        last = nc.tensor.matmul(to[:], hT[0:fn, n, c, j * P:(j + 1) * P], w2_share[0:fn, n, c], start=False,
                                                stop=n == TOP - 1 and c == NF - 1)
                last.then_inc(ffn_done, 1)

    @block.vector
    def _(dve):
        nc.vector.memset(logits[:], -3.0e38).then_inc(pads_ready, 1)
        dve.sem_inc(x1_ready, 2)
        dve.wait_ge(pads_ready, 1)
        with dve.Fori(0, B) as b:
            for j in range(J):
                p = j % 2
                n = b * J + j
                dve.wait_ge(attn_done, b * J + (j + 1))
                dve.wait_ge(tile_loaded[p], b * (16 * J) + 32 * (j // 2 + 1))
                nc.vector.tensor_tensor(x1[:, j], bank[p][:], x_in[p][:], ALU.add).then_inc(x1_ready, 1)
                dve.wait_ge(x1_ready, b * J + (j + 3))
                nc.vector.bn_stats(stats[:], x1[:, j]).then_inc(ln_steps, 1)
                wait_apart(dve, ln_steps, b * (4 * J) + (4 * j + 1), dve_waits_passed)
                nc.vector.bn_aggr(mv[:], stats[:]).then_inc(ln_steps, 1)
                dve.wait_ge(ln_steps, b * (4 * J) + (4 * j + 4))
                if j >= 2:
                    dve.wait_ge(xn_transposed, b * J + (j - 1))
                nc.vector.tensor_scalar(xn[p][:], x1[:, j], mv[:, 0:1], rstd[:], ALU.subtract, ALU.mult).then_inc(xn_ready, 1)
            dve.wait_ge(xnT_ready, b * J + J)
            nc.vector.tensor_reduce(token_sum[:], xnT[:], AX_X, ALU.add).then_inc(token_sum_ready, 1)
            R = ROUTE_STEPS
            steps = [0]

            def chained(ins):
                ins.then_inc(route_steps, 1)
                steps[0] += 1
                wait_apart(dve, route_steps, b * R + steps[0], dve_waits_passed)

            dve.wait_ge(logits_done, b + 1)
            chained(nc.vector.tensor_scalar(logits[:, 0:E], bank[2][0:1, 0:E], 1.0 / T, None, ALU.mult))
            chained(nc.vector.max(top_val[:], logits[:]))
            nc.vector.max_index(top_idx[:], top_val[:], logits[:]).then_inc(choice_ready, 1)
            chained(nc.vector.tensor_scalar(neg_max[:], top_val[:, 0:1], -1.0, None, ALU.mult))
            dve.wait_ge(exps_ready, b * 2 + 2)
            chained(nc.vector.reciprocal(inv_sum[:], exp_sum[:]))
            chained(nc.vector.tensor_scalar(top_prob[:], top_exp[:], inv_sum[:], None, ALU.mult))
            chained(nc.vector.tensor_tensor(prob_sum[:], top_prob[:, 0:1], top_prob[:, 1:2], ALU.add))
            chained(nc.vector.reciprocal(inv_prob[:], prob_sum[:]))
            nc.vector.tensor_scalar(share[:], top_prob[:], inv_prob[:], None, ALU.mult).then_inc(share_ready, 1)
            dve.wait_ge(share_spread, b + 1)
            nc.vector.tensor_copy(share_all[:], bank[3][:, 0:TOP]).then_inc(mix_steps, 1)
            dve.wait_ge(experts_loaded, b * EXPERT_LOADS + EXPERT_LOADS)
            dve.wait_ge(mix_steps, b * 2 + 1)
            dve.wait_ge(share_ready, b + 1)
            nc.vector.tensor_scalar(b2_part[:], b2_row[:, 0], share[:, 0:1], None, ALU.mult).then_inc(mix_steps, 1)
            for n in range(TOP):
                nc.vector.tensor_scalar(w2_share[:, n, 0:2], w2[:, n, 0:2], share_all[:, n:n + 1], None, ALU.mult)
                nc.vector.tensor_scalar(w2_share[0:LAST, n, 2], w2[0:LAST, n, 2], share_all[0:LAST, n:n + 1], None, ALU.mult)
            dve.wait_ge(mix_steps, b * 2 + 2)
            nc.vector.scalar_tensor_tensor(b2_mix[:], b2_row[:, 1], share[:, 1:2], b2_part[:], ALU.mult,
                                           ALU.add).then_inc(w2_ready, 1)
            for j in range(J):
                dve.wait_ge(ffn_done, b * J + (j + 1))
                dve.wait_ge(out_stored[j % 2], b * (8 * J) + 16 * (j // 2 + 1))
                nc.vector.tensor_tensor(o_out[j % 2][:], bank[6 + j % 2][:], x1[:, j], ALU.add).then_inc(o_ready, 1)

    @block.scalar
    def _(act):
        for p in range(2):
            act.sem_inc(out_stored[p], 16)
        with act.Fori(0, B) as b:
            nc.scalar.preload_act_table_set("natural_log_exp_and_others")
            for j in range(J):
                act.wait_ge(ln_steps, b * (4 * J) + (4 * j + 2))
                nc.scalar.activation(log_var[:], mv[:, 1:2], ACT.Ln, bias=ln_eps[:, 0:1]).then_inc(ln_steps, 1)
                act.wait_ge(ln_steps, b * (4 * J) + (4 * j + 3))
                nc.scalar.activation(rstd[:], log_var[:], ACT.Exp, scale=-0.5).then_inc(ln_steps, 1)
                act.wait_ge(xn_transposed, b * J + (j + 1))
                nc.scalar.activation(xnT[:, :, j * P:(j + 1) * P], bank[2 + j % 2][:].rearrange("p (k t) -> p k t", k=KC),
                                     ACT.Copy).then_inc(xnT_ready, 1)
            act.wait_ge(route_steps, b * ROUTE_STEPS + 3)
            nc.scalar.activation(exps[:], logits[:, 0:E], ACT.Exp, bias=neg_max[:], accum_out=exp_sum[:]).then_inc(exps_ready, 1)
            nc.scalar.activation(top_exp[:], top_val[:, 0:TOP], ACT.Exp, bias=neg_max[:]).then_inc(exps_ready, 1)
            g = 0
            for t in range(HALVES):
                for n in range(TOP):
                    for c, (f0, fn) in enumerate(FCH):
                        act.wait_ge(h_done, b * GROUPS + (g + 1))
                        nc.scalar.activation(hT[0:fn, n, c, t * 512:(t + 1) * 512], bank[4 + g % 2][0:fn, :], ACT.Gelu,
                                             bias=b1_col[0:fn, n, c:c + 1]).then_inc(h_ready, 1)
                        g += 1
            for j in range(J):
                act.wait_ge(o_ready, b * J + (j + 1))
                act.dma_start(out[bass.ds(b, 1), j * P:(j + 1) * P, :].rearrange("a t d -> (a t) d"),
                              o_out[j % 2][:]).then_inc(out_stored[j % 2], 16)
        for p in range(2):
            act.wait_ge(out_stored[p], 16 + 16 * (B * J // 2))


_INS = ["hidden_states", "Wq", "Wk", "Wv", "conv_q", "conv_k", "conv_v", "Wf1", "Wf2", "Wb", "A_log", "dt_bias", "Wg",
        "bg", "norm_w", "Wo"]
_INS = ["L0_attn_" + n for n in _INS] + ["L0_ffn_" + n for n in ("gate_W", "W1", "b1", "W2", "b2")]


def kernel(**inputs):
    import numpy as _np
    import concourse.bacc as _bacc
    from concourse import mybir as _mybir
    from concourse.bass_utils import run_bass_kernel_spmd as _run

    nc = _bacc.Bacc("TRN2", target_bir_lowering=False, num_devices=1)
    arrays, args = {}, []
    for name in _INS:
        a = _np.ascontiguousarray(inputs[name])
        arrays[f"in_{name}"] = a
        args.append(nc.dram_tensor(f"in_{name}", a.shape, _mybir.dt.from_np(a.dtype), kind="ExternalInput").ap())
    shape = inputs["L0_attn_hidden_states"].shape
    args.append(nc.dram_tensor("out_0", shape, _mybir.dt.from_np(_np.dtype("float32")), kind="ExternalOutput").ap())
    preln_delta_moe(nc, *args)
    r = _run(nc, [arrays], core_ids=[0])
    return r.results[0]["out_0"]
```

```python
from contextlib import ExitStack

import concourse.bass as bass
from concourse import mybir

P = 128
F32 = mybir.dt.float32
F32R = mybir.dt.float32r
I32 = mybir.dt.int32
U32 = mybir.dt.uint32
ALU = mybir.AluOpType
ACT = mybir.ActivationFunctionType
AX_X = mybir.AxisListType.X


class Step:

    def __init__(self, par_a=None, a=None, ja=None, a_first=False, par_m=None, m=None, jm=None, m_first=False,
                 par_b=None, b=None, h=None, j=None, ends=False):
        self.par_a, self.a, self.ja, self.a_first = par_a, a, ja, a_first
        self.par_m, self.m, self.jm, self.m_first = par_m, m, jm, m_first
        self.par_b, self.b, self.h, self.j, self.ends = par_b, b, h, j, ends


class Signal:

    def __init__(self, sem, per):
        self.sem, self.per = sem, per

    def at(self, unit, k):
        return unit * self.per + k


def wait_apart(eng, sem, value, passed):
    eng.wait_ge(sem, value)
    eng.sem_inc(passed, 1)


def preln_delta_moe(nc, x, Wq, Wk, Wv, conv_q, conv_k, conv_v, Wf1, Wf2, Wb, A_log, dt_bias, Wg, bg,
                    norm_w, Wo, gate_W, W1, b1, W2, b2, out):
    B, T, D = x.shape
    H = A_log.shape[0]
    HC = Wq.shape[1]
    NG = Wf2.shape[1] // H
    GG = P // NG
    KC = D // P
    J = T // P
    UC = B * P
    TAPS = conv_q.shape[1]
    HALO = TAPS - 1
    LEVELS = 7
    SCALE = float(P) ** -0.5
    L2_EPS, LN_EPS = 1e-6, 1e-5
    E, _, FF = W1.shape
    FCH = [(0, 128), (128, 128), (256, FF - 256)]
    NF = len(FCH)
    assert HC == H * P and UC == 512 and H * NG == P and H % 2 == 0 and J % 2 == 0 and J > 2 and 256 < FF <= 384
    GRAIN = 2.0 ** 46
    assert 1 << LEVELS == P

    y_scratch = nc.dram_tensor("y_scratch", [J, B, P, H, P], F32, kind="Internal").ap()
    beta_scratch = nc.dram_tensor("beta_scratch", [H, J, UC], F32, kind="Internal").ap()
    decay_scratch = nc.dram_tensor("decay_scratch", [H, NG, J, UC], F32, kind="Internal").ap()

    with ExitStack() as whole:
        bank = [whole.enter_context(nc.psum_tensor(f"bank{i}", [P, 512], F32)) for i in range(8)]
        ident = whole.enter_context(nc.sbuf_tensor("ident", [P, P], F32))
        ones = whole.enter_context(nc.sbuf_tensor("ones", [P, P], F32))
        ln_eps = whole.enter_context(nc.sbuf_tensor("ln_eps", [P, 1], F32))
        with ExitStack() as ctx:
            attention(nc, ctx, locals())
        with ExitStack() as ctx:
            mixture(nc, ctx, locals())


def attention(nc, ctx, env):
    (x, Wq, Wk, Wv, Wg, conv_q, conv_k, conv_v, Wf1, Wf2, Wb, A_log, dt_bias, bg, norm_w) = (env[n] for n in (
        "x", "Wq", "Wk", "Wv", "Wg", "conv_q", "conv_k", "conv_v", "Wf1", "Wf2", "Wb", "A_log", "dt_bias", "bg",
        "norm_w"))
    (B, T, D, H, NG, GG, KC, J, UC, TAPS, HALO, LEVELS, SCALE, L2_EPS, LN_EPS, GRAIN) = (env[n] for n in (
        "B", "T", "D", "H", "NG", "GG", "KC", "J", "UC", "TAPS", "HALO", "LEVELS", "SCALE", "L2_EPS", "LN_EPS", "GRAIN"))
    y_scratch, beta_scratch, decay_scratch = env["y_scratch"], env["beta_scratch"], env["decay_scratch"]
    bank, ident, ones, ln_eps = env["bank"], env["ident"], env["ones"], env["ln_eps"]

    def sb(name, shape, dt=F32):
        return ctx.enter_context(nc.sbuf_tensor(name, shape, dt))

    def sem(name):
        return ctx.enter_context(nc.semaphore(name))

    def signal(name, per):
        return Signal(sem(name), per)

    xT = sb("xT", [P, KC, J * UC])
    mean_ones = sb("mean_ones", [P, P])
    level_mask = sb("level_mask", [P, LEVELS, UC // 2])
    pairs = sb("pairs", [P, LEVELS, UC], F32R)
    all_pairs = sb("all_pairs", [P, 2, UC])
    state = sb("state", [P, UC])
    ident_r = sb("ident_r", [P, P], F32R)
    ones_r = sb("ones_r", [P, P], F32R)
    ident_each = sb("ident_each", [P, UC])
    ZI = sb("ZI", [P, LEVELS - 1, UC], F32R)
    norm_w_col = sb("norm_w_col", [P, 1])
    l2_eps = sb("l2_eps", [P, 1])

    with ExitStack() as c0:
        def sb0(name, shape, dt=F32):
            return c0.enter_context(nc.sbuf_tensor(name, shape, dt))

        def sem0(name):
            return c0.enter_context(nc.semaphore(name))

        wf1 = sb0("wf1", [P, KC, P])
        wf2 = sb0("wf2", [P, P])
        wb = sb0("wb", [P, KC, H])
        dt_col = sb0("dt_col", [P, 1])
        alog_col = sb0("alog_col", [P, 1])
        rate_col = sb0("rate_col", [P, 1])
        xt = [sb0(f"xt{p}", [P, B, D]) for p in range(2)]
        stats = sb0("stats", [P, B, 6])
        mv = sb0("mv", [P, B, 2])
        log_var = sb0("log_var", [P, B])
        rstd = sb0("rstd", [P, B])
        f1_sb = sb0("f1_sb", [P, UC])
        b_exp = sb0("b_exp", [H, UC])
        b_den = sb0("b_den", [H, UC])
        b_out = sb0("b_out", [H, UC])
        z = sb0("z", [P, UC])
        z_abs = sb0("z_abs", [P, UC])
        z_exp = sb0("z_exp", [P, UC])
        z_s = sb0("z_s", [P, UC])
        z_s2 = sb0("z_s2", [P, UC])
        z_sum = sb0("z_sum", [P, UC])
        softplus = sb0("softplus", [P, UC])
        decay = sb0("decay", [P, UC])

        consts_loaded = sem0("consts_loaded")
        x_loaded = [sem0(f"x_loaded{p}") for p in range(2)]
        pool_steps = sem0("pool_steps")
        ln_steps = sem0("ln_steps")
        xn_ready = sem0("xn_ready")
        x_transposed = sem0("x_transposed")
        xT_ready = sem0("xT_ready")
        beta_logits_done = sem0("beta_logits_done")
        beta_exp_ready = sem0("beta_exp_ready")
        beta_steps = sem0("beta_steps")
        f1_done = sem0("f1_done")
        f1_ready = sem0("f1_ready")
        f2_done = sem0("f2_done")
        sp_act_steps = sem0("sp_act_steps")
        sp_vec_steps = sem0("sp_vec_steps")
        softplus_ready = sem0("softplus_ready")
        rate_steps = sem0("rate_steps")
        z_exp_ready = sem0("z_exp_ready")
        waits_passed0 = sem0("waits_passed0")
        decay_ready = sem0("decay_ready")
        scratch_stored = sem0("scratch_stored")
        NCONST = 5 + NG
        ATANH = [2.0 / n for n in range(1, 16, 2)]
        SP_STEPS = 4 + len(ATANH)

        block = c0.enter_context(nc.Block())

        @block.sync
        def _(sp):
            x_chunks = x.rearrange("b (j t) d -> j t b d", t=P)
            for p in range(2):
                sp.dma_start(xt[p][:], x_chunks[p]).then_inc(x_loaded[p], 16)
            sp.dma_start(wf1[:], Wf1.rearrange("(k p) f -> p k f", p=P)).then_inc(consts_loaded, 16)
            sp.dma_start(wf2[:], Wf2).then_inc(consts_loaded, 16)
            sp.dma_start(wb[:], Wb.rearrange("(k p) h -> p k h", p=P)).then_inc(consts_loaded, 16)
            sp.dma_start(dt_col[:], dt_bias.rearrange("(c o) -> c o", o=1)).then_inc(consts_loaded, 16)
            sp.dma_start(norm_w_col[:], norm_w.rearrange("(c o) -> c o", o=1)).then_inc(consts_loaded, 16)
            for g in range(NG):
                sp.dma_start(alog_col[g::NG, :], A_log.rearrange("(c o) -> c o", o=1)).then_inc(consts_loaded, 16)
            sp.sem_inc(scratch_stored, 32)

            def store(j):
                sp.wait_ge(beta_steps, j * 2 + 2)
                sp.dma_start(beta_scratch[:, bass.ds(j, 1), :].rearrange("h a c -> h (a c)"),
                             b_out[:]).then_inc(scratch_stored, 16)
                sp.wait_ge(decay_ready, j + 1)
                sp.dma_start(decay_scratch.rearrange("h g j c -> (h g) j c")[:, bass.ds(j, 1), :]
                             .rearrange("h a c -> h (a c)"), decay[:]).then_inc(scratch_stored, 16)

            with sp.Fori(0, J // 2 - 1) as jj:
                for p in range(2):
                    j = sp.snap(jj * 2 + p)
                    sp.wait_ge(x_transposed, j * KC + KC)
                    sp.dma_start(xt[p][:], x_chunks[bass.ds(j + 2, 1)].rearrange("a t b d -> (a t) b d")) \
                        .then_inc(x_loaded[p], 16)
                    store(j)
            for j in range(J - 2, J):
                store(j)
            sp.wait_ge(scratch_stored, 32 * (J + 1))

        @block.gpsimd
        def _(pool):
            nc.gpsimd.memset(ident[:], 0.0).then_inc(pool_steps, 1)
            pool.wait_ge(pool_steps, 1)
            nc.gpsimd.affine_select(out=ident[:], in_=ident[:], compare_op=ALU.not_equal, fill=1.0, base=0,
                                    pattern=[[-1, P]], channel_multiplier=1).then_inc(pool_steps, 1)
            nc.gpsimd.memset(ones[:], 1.0)
            nc.gpsimd.memset(mean_ones[:], 1.0 / P)
            nc.gpsimd.memset(ln_eps[:], LN_EPS)
            nc.gpsimd.memset(l2_eps[:], L2_EPS)
            nc.gpsimd.memset(level_mask[:], GRAIN).then_inc(pool_steps, 1)
            nc.gpsimd.memset(all_pairs[:, 1], 0.0)
            nc.gpsimd.memset(state[:], 0.0)
            pool.wait_ge(pool_steps, 3)
            nc.gpsimd.tensor_copy(ident_r[:], ident[:])
            nc.gpsimd.tensor_copy(ones_r[:], ones[:])
            each = ident[:].unsqueeze(1).to_broadcast([P, B, P])
            nc.gpsimd.tensor_copy(ident_each[:].rearrange("p (b t) -> p b t", b=B), each)
            nc.gpsimd.tensor_scalar(all_pairs[:, 0].rearrange("p (b t) -> p b t", b=B), each, -1.0, None, ALU.mult)
            for l in range(LEVELS - 1):
                nc.gpsimd.tensor_copy(ZI[:, l].rearrange("p (b t) -> p b t", b=B), each)
            for l in range(LEVELS):
                nc.gpsimd.tensor_scalar(pairs[:, l].rearrange("p (b t) -> p b t", b=B), each, 0.0, None, ALU.mult)
            for l in range(LEVELS):
                half, blocks = 1 << l, P >> (l + 1)
                m = level_mask[:, l, :].rearrange("p (b m s) -> p b m s", b=B, m=blocks)
                nc.gpsimd.affine_select(out=m, in_=m, compare_op=ALU.is_ge, fill=0.0, base=0,
                                        pattern=[[0, B], [-2 * half, blocks], [0, half]],
                                        channel_multiplier=1).then_inc(pool_steps, 1)
                pool.wait_ge(pool_steps, 4 + 2 * l)
                nc.gpsimd.affine_select(out=m, in_=m, compare_op=ALU.is_ge, fill=0.0, base=half - 1,
                                        pattern=[[0, B], [2 * half, blocks], [0, half]],
                                        channel_multiplier=-1).then_inc(pool_steps, 1)

        @block.vector
        def _(dve):
            dve.wait_ge(rate_steps, 1)
            nc.vector.tensor_scalar(rate_col[:], alog_col[:], -1.0, None, ALU.mult).then_inc(rate_steps, 1)

            def layer_norm(j, p, loads):
                dve.wait_ge(x_loaded[p], loads)
                for b in range(B):
                    last = nc.vector.bn_stats(stats[:, b, :], xt[p][:, b, :])
                last.then_inc(ln_steps, 1)
                wait_apart(dve, ln_steps, j * 4 + 1, waits_passed0)
                if not isinstance(j, int) or j > 0:
                    wait_apart(dve, xn_ready, j, waits_passed0)
                for b in range(B):
                    last = nc.vector.bn_aggr(mv[:, b, :], stats[:, b, :])
                last.then_inc(ln_steps, 1)
                dve.wait_ge(ln_steps, j * 4 + 4)
                for b in range(B):
                    last = nc.vector.tensor_scalar(xt[p][:, b, :], xt[p][:, b, :], mv[:, b, 0:1], rstd[:, b:b + 1],
                                                   ALU.subtract, ALU.mult)
                last.then_inc(xn_ready, 1)

            def gates(j):
                dve.wait_ge(beta_exp_ready, j + 1)
                nc.vector.tensor_scalar(b_den[:], b_exp[:], 1.0, None, ALU.add).then_inc(beta_steps, 1)
                dve.wait_ge(beta_steps, j * 2 + 1)
                dve.wait_ge(scratch_stored, j * 32 + 32)
                nc.vector.reciprocal(b_out[:], b_den[:]).then_inc(beta_steps, 1)
                n = j * SP_STEPS

                def chained(k, ins):
                    ins.then_inc(sp_vec_steps, 1)
                    dve.wait_ge(sp_vec_steps, n + k)

                dve.wait_ge(z_exp_ready, j + 1)
                chained(1, nc.vector.tensor_scalar(z_s[:], z_exp[:], 2.0, None, ALU.add))
                chained(2, nc.vector.reciprocal(z_s[:], z_s[:]))
                chained(3, nc.vector.tensor_tensor(z_s[:], z_s[:], z_exp[:], ALU.mult))
                chained(4, nc.vector.tensor_tensor(z_s2[:], z_s[:], z_s[:], ALU.mult))
                chained(5, nc.vector.tensor_scalar(z_sum[:], z_s2[:], ATANH[-1], None, ALU.mult))
                for k, c in enumerate(ATANH[-2:0:-1]):
                    chained(6 + k, nc.vector.scalar_tensor_tensor(z_sum[:], z_sum[:], c, z_s2[:], ALU.add, ALU.mult))
                chained(SP_STEPS, nc.vector.scalar_tensor_tensor(z_sum[:], z_sum[:], ATANH[0], z_s[:], ALU.add, ALU.mult))
                nc.vector.scalar_tensor_tensor(softplus[:], z[:], 0.0, z_sum[:], ALU.max,
                                               ALU.add).then_inc(softplus_ready, 1)

            layer_norm(0, 0, 16)
            with dve.Fori(0, J // 2 - 1) as jj:
                for p in range(2):
                    j = dve.snap(jj * 2 + p)
                    layer_norm(j + 1, 1 - p, jj * 16 + 16 * (p + 1))
                    gates(j)
            layer_norm(J - 1, 1, 8 * J)
            gates(J - 2)
            gates(J - 1)

        @block.scalar
        def _(act):
            nc.scalar.preload_act_table_set("natural_log_exp_and_others")
            act.wait_ge(consts_loaded, 16 * NCONST)
            nc.scalar.activation(alog_col[:], alog_col[:], ACT.Exp).then_inc(rate_steps, 1)
            act.wait_ge(rate_steps, 2)
            act.wait_ge(pool_steps, 3)

            def inverse_std(j):
                act.wait_ge(ln_steps, j * 4 + 2)
                nc.scalar.activation(log_var[:], mv[:, :, 1], ACT.Ln, bias=ln_eps[:, 0:1]).then_inc(ln_steps, 1)
                act.wait_ge(ln_steps, j * 4 + 3)
                nc.scalar.activation(rstd[:], log_var[:], ACT.Exp, scale=-0.5).then_inc(ln_steps, 1)

            def chunk(j, first):
                for k in range(KC):
                    act.wait_ge(x_transposed, j * KC + (k + 1))
                    nc.scalar.activation(xT[:, k, bass.ds(j * UC, UC)], bank[k][:], ACT.Copy).then_inc(xT_ready, 1)
                act.wait_ge(beta_logits_done, j + 1)
                if not first:
                    act.wait_ge(beta_steps, j * 2 - 1)
                nc.scalar.activation(b_exp[:], bank[5][0:H, :], ACT.Exp, scale=-1.0).then_inc(beta_exp_ready, 1)
                act.wait_ge(f1_done, j + 1)
                nc.scalar.activation(f1_sb[:], bank[4][:], ACT.Copy).then_inc(f1_ready, 1)
                if not first:
                    decays(j - 1)
                act.wait_ge(f2_done, j + 1)
                nc.scalar.activation(z[:], bank[6][:], ACT.Identity, bias=dt_col[:, 0:1]).then_inc(sp_act_steps, 1)
                act.wait_ge(sp_act_steps, j * 2 + 1)
                nc.scalar.activation(z_abs[:], z[:], ACT.Abs).then_inc(sp_act_steps, 1)
                act.wait_ge(sp_act_steps, j * 2 + 2)
                nc.scalar.activation(z_exp[:], z_abs[:], ACT.Exp, scale=-1.0).then_inc(z_exp_ready, 1)

            def decays(j):
                act.wait_ge(softplus_ready, j + 1)
                act.wait_ge(scratch_stored, j * 32 + 32)
                nc.scalar.activation(decay[:], softplus[:], ACT.Exp, scale=rate_col[:, 0:1]).then_inc(decay_ready, 1)

            inverse_std(0)
            chunk(0, True)
            inverse_std(1)
            with act.Fori(0, J - 2) as jj:
                j = act.snap(jj + 1)
                chunk(j, False)
                inverse_std(j + 1)
            chunk(J - 1, False)
            decays(J - 1)

        @block.tensor
        def _(pe):
            pe.wait_ge(pool_steps, 2)
            pe.wait_ge(consts_loaded, 16 * NCONST)
            with pe.Fori(0, J // 2) as jj:
                for p in range(2):
                    j = pe.snap(jj * 2 + p)
                    pe.wait_ge(xn_ready, j + 1)
                    for k in range(KC):
                        for b in range(B):
                            last = nc.tensor.transpose(bank[k][:, b * P:(b + 1) * P], xt[p][:, b, k * P:(k + 1) * P],
                                                       ident[:])
                        last.then_inc(x_transposed, 1)
                    pe.wait_ge(xT_ready, j * KC + KC)
                    for k in range(KC):
                        last = nc.tensor.matmul(bank[5][0:H, :], wb[:, k, :], xT[:, k, bass.ds(j * UC, UC)],
                                                start=k == 0, stop=k == KC - 1)
                    last.then_inc(beta_logits_done, 1)
                    for k in range(KC):
                        last = nc.tensor.matmul(bank[4][:], wf1[:, k, :], xT[:, k, bass.ds(j * UC, UC)],
                                                start=k == 0, stop=k == KC - 1)
                    last.then_inc(f1_done, 1)
                    pe.wait_ge(f1_ready, j + 1)
                    nc.tensor.matmul(bank[6][:], wf2[:], f1_sb[:], start=True, stop=True).then_inc(f2_done, 1)

    weights = [sb(f"weights{p}", [P, 4, KC, P]) for p in range(2)]
    taps = [sb(f"taps{p}", [P, 3, TAPS]) for p in range(2)]
    bg_col = [sb(f"bg_col{p}", [P, 1]) for p in range(2)]
    pre = sb("pre", [P, 3, B, HALO + P])
    conv = sb("conv", [P, 3, B, P])
    silu = sb("silu", [P, 2, UC])
    v_u = sb("v_u", [P, UC])
    gate = sb("gate", [P, UC])
    squares = sb("squares", [P, 2, UC], F32R)
    squares_rest = sb("squares_rest", [P, 2, UC], F32R)
    rnorm = sb("rnorm", [P, 2, UC])
    decay_u = sb("decay_u", [P, UC])
    beta_u = sb("beta_u", [P, UC])
    k_hat = sb("k_hat", [P, UC])
    q_hat = sb("q_hat", [P, UC])
    KQ = sb("KQ", [P, 2, UC])
    KQ_scan = sb("KQ_scan", [P, 2, UC])
    KR = sb("KR", [P, UC])
    total = [decay_u] + [sb(f"total{l}", [P, UC >> l]) for l in range(1, LEVELS + 1)]
    X = sb("X", [P, UC], F32R)
    T_inv = sb("T_inv", [P, UC], F32R)
    k_rows = sb("k_rows", [P, UC])
    pairs_scan = sb("pairs_scan", [P, 2, UC])
    chunk_decay = sb("chunk_decay", [P, B])
    U_sb = sb("U_sb", [P, UC])
    U_r = sb("U_r", [P, UC], F32R)
    residual = sb("residual", [P, UC], F32R)
    delta = sb("delta", [P, UC])
    yg = sb("yg", [P, UC])
    y_sq = sb("y_sq", [P, UC])
    y_rn = sb("y_rn", [P, UC])
    y_out = sb("y_out", [P, UC])

    HEAD_LOADS = 8
    REFINEMENTS = 2
    dve_waits_passed, pool_waits_passed = sem("dve_waits_passed"), sem("pool_waits_passed")
    head_loaded = sem("head_loaded")
    unit_loaded = signal("unit_loaded", 32)
    y_stored = sem("y_stored")
    qk_projected = signal("qk_projected", 2)
    v_projected = signal("v_projected", 1)
    gate_projected = signal("gate_projected", 1)
    sums_done = signal("sums_done", 2)
    diag_done = signal("diag_done", 1)
    level_done = signal("level_done", LEVELS)
    z_done = signal("z_done", LEVELS - 1)
    x_done = signal("x_done", LEVELS - 1)
    t_done = signal("t_done", LEVELS - 1)
    k_transposed = signal("k_transposed", 1)
    u_done = signal("u_done", 1)
    product_done = signal("product_done", REFINEMENTS)
    correction_done = signal("correction_done", REFINEMENTS)
    o_state_done = signal("o_state_done", 1)
    delta_done = signal("delta_done", 1)
    o_done = signal("o_done", 1)
    s_done = signal("s_done", 1)
    y_sums_done = signal("y_sums_done", 1)
    qk_halo_ready, v_halo_ready = signal("qk_halo_ready", 1), signal("v_halo_ready", 1)
    qk_conv_steps, v_conv_steps = signal("qk_conv_steps", 2 * TAPS), signal("v_conv_steps", TAPS)
    state_ready = signal("state_ready", 1)
    chunk_decay_ready = signal("chunk_decay_ready", 1)
    residual_ready = signal("residual_ready", REFINEMENTS)
    delta_refined = signal("delta_refined", REFINEMENTS)
    hats_ready = signal("hats_ready", 1)
    unit_ready = signal("unit_ready", 1)
    scaled = signal("scaled", LEVELS)
    pairs_ready = signal("pairs_ready", LEVELS + 1)
    t1_ready = signal("t1_ready", 1)
    x1_ready = signal("x1_ready", 1)
    zi_ready = signal("zi_ready", LEVELS - 1)
    yg_ready = signal("yg_ready", 1)
    y_ready = signal("y_ready", 1)
    qk_pre_ready, v_pre_ready = signal("qk_pre_ready", 2), signal("v_pre_ready", 1)
    scan_ready = signal("scan_ready", 1)
    pairs_kept = signal("pairs_kept", 1)
    silu_ready = signal("silu_ready", 2)
    squares_ready = signal("squares_ready", 2)
    v_silu_ready = signal("v_silu_ready", 1)
    sums_taken = signal("sums_taken", 2)
    rnorm_ready = signal("rnorm_ready", 2)
    y_sums_free = sem("y_sums_free")
    y_rn_ready = signal("y_rn_ready", 1)
    gate_ready = signal("gate_ready", 1)
    x_ready = signal("x_ready", LEVELS - 1)
    t_ready = signal("t_ready", LEVELS - 2)
    k_rows_ready = signal("k_rows_ready", 1)
    u_ready = signal("u_ready", 1)
    u_kept = signal("u_kept", 1)
    delta_ready = signal("delta_ready", 1)
    y_sq_ready = signal("y_sq_ready", 1)
    square_ready = signal("square_ready", 2)
    squares_rest_ready = signal("squares_rest_ready", 2)
    keys_scaled = signal("keys_scaled", LEVELS)

    def wait(eng, sig, unit, k):
        eng.wait_ge(sig.sem, sig.at(unit, k))

    def cols(b):
        return slice(b * P, (b + 1) * P)

    def half_cols(b):
        return slice(b * (P // 2), (b + 1) * (P // 2))

    def halves(ap, l, which):
        if len(ap.shape) == 2:
            return ap.rearrange("p (m two s) -> p m two s", two=2, s=1 << l)[:, :, which, :]
        return ap.rearrange("p k (m two s) -> p k m two s", two=2, s=1 << l)[:, :, :, which, :]

    def by_batch(ap):
        return ap.rearrange("p (b t) -> p b t", b=B)

    def on_each_batch(ap):
        return ap.unsqueeze(1).to_broadcast([P, B, P])

    def walk(eng, step):
        step(Step(par_a=0, a=0, ja=0, a_first=True))
        step(Step(par_a=0, a=1, ja=1, par_m=0, m=0, jm=0, m_first=True))

        def head(h, par, last):
            with eng.Fori(0, J - 2) as j:
                b = eng.snap(h * J + j)
                step(Step(par_a=par, a=b + 2, ja=j + 2, par_m=par, m=b + 1, jm=j + 1, par_b=par, b=b, h=h, j=j))
            b = h * J + (J - 2) if isinstance(h, int) else eng.snap(h * J + (J - 2))
            if last:
                step(Step(par_m=par, m=b + 1, jm=J - 1, par_b=par, b=b, h=h, j=J - 2))
                step(Step(par_b=par, b=b + 1, h=h, j=J - 1, ends=True))
            else:
                step(Step(par_a=1 - par, a=b + 2, ja=0, a_first=True, par_m=par, m=b + 1, jm=J - 1, par_b=par, b=b, h=h,
                          j=J - 2))
                b = b + 1 if isinstance(h, int) else eng.snap(h * J + (J - 1))
                step(Step(par_a=1 - par, a=b + 2, ja=1, par_m=1 - par, m=b + 1, jm=0, m_first=True, par_b=par, b=b, h=h,
                          j=J - 1, ends=True))

        with eng.Fori(0, H // 2 - 1) as hp:
            for par in range(2):
                head(hp * 2 + par, par, False)
        head(H - 2, 0, False)
        head(H - 1, 1, True)

    block = ctx.enter_context(nc.Block())

    @block.sync
    def _(sp):
        def load_head(h, par):
            at = bass.ds(h * P, P)
            for m, W in enumerate((Wq, Wk, Wv, Wg)):
                sp.dma_start(weights[par][:, m, :, :], W.rearrange("(k p) n -> p k n", p=P)[:, :, at]) \
                    .then_inc(head_loaded, 16)
            for m, c in enumerate((conv_q, conv_k, conv_v)):
                sp.dma_start(taps[par][:, m, :], c[at, :]).then_inc(head_loaded, 16)
            sp.dma_start(bg_col[par][:], bg.rearrange("(c o) -> c o", o=1)[at, :]).then_inc(head_loaded, 16)

        def load_unit(h, j):
            sp.dma_start(beta_u[:], beta_scratch[bass.ds(h, 1), bass.ds(j, 1), :].rearrange("a b c -> (a b) c")
                         .to_broadcast([P, UC])).then_inc(unit_loaded.sem, 16)
            rows = decay_scratch[bass.ds(h, 1), :, bass.ds(j, 1), :].rearrange("a g b c -> (a g) (b c)")
            sp.dma_start(decay_u[:], rows.unsqueeze(1).to_broadcast([NG, GG, UC])).then_inc(unit_loaded.sem, 16)

        load_head(0, 0)
        load_unit(0, 0)

        def decays_used(u):
            wait(sp, scaled, u, 1)
            wait(sp, keys_scaled, u, 1)

        def head(h, par, last):
            with sp.Fori(0, J - 1) as j:
                decays_used(sp.snap(h * J + j))
                load_unit(h, j + 1)
            if not last:
                decays_used(h * J + J - 1 if isinstance(h, int) else sp.snap(h * J + (J - 1)))
                load_unit(h + 1, 0)

        def load_next(h, par):
            wait(sp, gate_ready, h * J - 1, 1)
            wait(sp, v_conv_steps, h * J - 1, TAPS)
            load_head(h + 1, 1 - par)

        sp.wait_ge(head_loaded, 16 * HEAD_LOADS)
        load_head(1, 1)
        head(0, 0, False)
        with sp.Fori(0, H // 2 - 1) as hp:
            load_next(hp * 2 + 1, 1)
            head(hp * 2 + 1, 1, False)
            load_next(hp * 2 + 2, 0)
            head(hp * 2 + 2, 0, False)
        head(H - 1, 1, True)

    @block.tensor
    def _(pe):
        def step(s):
            a, m, b = s.a, s.m, s.b

            def project(w, ks):
                u, par, j, done = (a, s.par_a, s.ja, qk_projected) if w < 2 else \
                    (m, s.par_m, s.jm, (v_projected, gate_projected)[w - 2])
                if u is None:
                    return
                if ks[0] == 0:
                    if w == 0 and s.a_first:
                        pe.wait_ge(head_loaded, a * (16 * HEAD_LOADS // J) + 16 * HEAD_LOADS)
                    if w < 2:
                        if b is not None:
                            wait(pe, v_pre_ready if w == 0 else gate_ready, b, 1)
                        elif m is not None:
                            wait(pe, qk_pre_ready, m, w + 1)
                    elif a is not None:
                        wait(pe, qk_pre_ready, a, w - 1)
                    elif w == 2:
                        wait(pe, v_pre_ready, b, 1)
                    else:
                        wait(pe, gate_ready, b, 1)
                for k in ks:
                    last = nc.tensor.matmul(bank[w % 2][:], weights[par][:, w, k, :], xT[:, k, bass.ds(j * UC, UC)],
                                            start=k == 0, stop=k == KC - 1)
                if ks[-1] == KC - 1:
                    last.then_inc(done.sem, 1)

            def diagonal():
                if m is None:
                    return
                wait(pe, unit_ready, m, 1)
                if b is not None:
                    wait(pe, k_rows_ready, b, 1)
                for i in range(B):
                    last = nc.tensor.matmul(bank[4][:, cols(i)], KR[:, cols(i)], q_hat[:, cols(i)], start=True, stop=True)
                last.then_inc(diag_done.sem, 1)

            def level(l):
                if m is None:
                    return
                if l == 0:
                    wait(pe, unit_ready, m, 1)
                else:
                    wait(pe, scaled, m, l)
                    wait(pe, keys_scaled, m, l)
                    wait(pe, pairs_ready, m, l)
                to = bank[3 + l % 2][:].rearrange("p (k b m s) -> p k b m s", k=2, b=B, s=1 << l)
                for i in range(B):
                    last = nc.tensor.matmul(to[:, :, i], KR[:, cols(i)], halves(KQ[:, :, cols(i)], l, 1),
                                            start=True, stop=True)
                last.then_inc(level_done.sem, 1)

            def transpose_pairs():
                if m is None:
                    return
                wait(pe, pairs_ready, m, LEVELS + 1)
                pe.wait_ge(state_ready.sem, m + 1)
                for i in range(B):
                    last = nc.tensor.matmul(bank[7][:, cols(i)], pairs[:, 0, cols(i)], ident_r[:], start=True, stop=True)
                last.then_inc(t_done.sem, 1)

            def inverse_z(l):
                if b is None:
                    return
                if l == 1:
                    wait(pe, t1_ready, b, 1)
                else:
                    wait(pe, t_ready, b, l - 1)
                for i in range(B):
                    last = nc.tensor.matmul(bank[5][:, half_cols(i)], pairs[:, l, cols(i)], halves(T_inv[:, cols(i)], l, 0),
                                            start=True, stop=True)
                last.then_inc(z_done.sem, 1)

            def inverse_xt(l):
                if b is None:
                    return
                wait(pe, zi_ready, b, l)
                if l >= 2:
                    wait(pe, x_ready, b, l - 1)
                else:
                    wait(pe, x1_ready, b, 1)
                if l < LEVELS - 1:
                    for i in range(B):
                        last = nc.tensor.matmul(bank[7][:, half_cols(i)], X[:, cols(i)], halves(ZI[:, l - 1, cols(i)], l, 0),
                                                start=True, stop=True)
                    last.then_inc(t_done.sem, 1)
                for i in range(B):
                    last = nc.tensor.matmul(bank[6][:, half_cols(i)], ZI[:, l - 1, cols(i)], halves(X[:, cols(i)], l, 1),
                                            start=True, stop=True)
                last.then_inc(x_done.sem, 1)

            def sums(which):
                if a is None:
                    return
                wait(pe, squares_rest_ready, a, which + 1)
                if which == 1:
                    wait(pe, sums_taken, a, 1)
                elif m is not None:
                    wait(pe, sums_taken, m, 2)
                    if b is not None:
                        pe.wait_ge(y_sums_free, b + 1)
                nc.tensor.matmul(bank[2][:], ones_r[:], squares[:, which, :], start=True, stop=False)
                nc.tensor.matmul(bank[2][:], ones_r[:], squares_rest[:, which, :], start=False,
                                 stop=True).then_inc(sums_done.sem, 1)

            def apply_inverse(to):
                for i in range(B):
                    last = nc.tensor.matmul(bank[5][:, cols(i)], X[:, cols(i)], to[:, cols(i)], start=True, stop=True)
                return last

            def refine(n):
                if b is None:
                    return
                if n == 0:
                    wait(pe, u_kept, b, 1)
                    wait(pe, pairs_kept, b, 1)
                    wait(pe, delta_ready, b, 1)
                else:
                    wait(pe, delta_refined, b, n)
                for i in range(B):
                    last = nc.tensor.matmul(bank[7][:, cols(i)], pairs_scan[:, 0, cols(i)], delta[:, cols(i)], start=True,
                                            stop=True)
                last.then_inc(product_done.sem, 1)

            def correct_by_residual(n):
                if b is None:
                    return
                wait(pe, residual_ready, b, n + 1)
                apply_inverse(residual).then_inc(correction_done.sem, 1)

            project(0, range(KC))
            inverse_z(1)
            diagonal()
            level(0)
            inverse_xt(1)
            project(1, (0,))
            inverse_z(2)
            project(1, (1,))
            level(1)
            inverse_xt(2)
            project(1, (2,))
            inverse_z(3)
            project(1, (3,))
            level(2)
            inverse_xt(3)
            project(2, (0,))
            inverse_z(4)
            project(2, (1,))
            level(3)
            inverse_xt(4)
            project(2, (2,))
            inverse_z(5)
            project(2, (3,))
            level(4)
            inverse_xt(5)
            project(3, (0,))
            inverse_z(6)
            if b is not None:
                wait(pe, v_silu_ready, b, 1)
                wait(pe, scan_ready, b, 1)
                for i in range(B):
                    nc.tensor.matmul(bank[7][:, cols(i)], v_u[:, cols(i)], ident[:], start=True, stop=False)
                    last = nc.tensor.matmul(bank[7][:, cols(i)], KQ_scan[:, 0, cols(i)], state[:, cols(i)], start=False,
                                            stop=True)
                last.then_inc(u_done.sem, 1)
            level(5)
            inverse_xt(6)
            project(3, (1,))
            if b is not None:
                wait(pe, x_ready, b, LEVELS - 1)
                for i in range(B):
                    last = nc.tensor.matmul(bank[6][:, cols(i)], state[:, cols(i)], KQ_scan[:, 1, cols(i)], start=i == 0,
                                            stop=False, skip_group_check=True)
                last.then_inc(o_state_done.sem, 1)
            if b is not None:
                wait(pe, u_ready, b, 1)
                apply_inverse(U_r).then_inc(delta_done.sem, 1)
            sums(0)
            refine(0)
            level(6)
            correct_by_residual(0)
            project(3, (2,))
            refine(1)
            sums(1)
            correct_by_residual(1)
            project(3, (3,))
            if b is not None:
                wait(pe, delta_refined, b, REFINEMENTS)
                for i in range(B):
                    last = nc.tensor.matmul(bank[6][:, cols(i)], delta[:, cols(i)], pairs_scan[:, 1, cols(i)], start=False,
                                            stop=i == B - 1, skip_group_check=True)
                last.then_inc(o_done.sem, 1)
                for i in range(B):
                    last = nc.tensor.matmul(bank[7][:, cols(i)], k_rows[:, cols(i)], delta[:, cols(i)], start=True, stop=True)
                last.then_inc(s_done.sem, 1)
            if m is not None:
                wait(pe, keys_scaled, m, LEVELS)
                wait(pe, pairs_ready, m, LEVELS)
                for i in range(B):
                    last = nc.tensor.transpose(bank[4][:, cols(i)], KR[:, cols(i)], ident[:])
                last.then_inc(k_transposed.sem, 1)
            if b is not None:
                if a is not None:
                    wait(pe, sums_taken, a, 2)
                wait(pe, y_sq_ready, b, 1)
                nc.tensor.matmul(bank[2][:], mean_ones[:], y_sq[:], start=True, stop=True).then_inc(y_sums_done.sem, 1)
            transpose_pairs()

        walk(pe, step)

    @block.vector
    def _(dve):
        dve.sem_inc(state_ready.sem, 1)

        def step(s):
            a, m, b = s.a, s.m, s.b

            def halo(u, first, before, steps, per, rows, ready):
                if u is None:
                    return
                if before is not None:
                    wait(dve, steps, before, per)
                if first:
                    nc.vector.memset(pre[:, rows, :, 0:HALO], 0.0).then_inc(ready.sem, 1)
                else:
                    nc.vector.tensor_copy(pre[:, rows, :, 0:HALO], pre[:, rows, :, P:P + HALO]).then_inc(ready.sem, 1)

            def convolve(w, which=range(TAPS)):
                u, before, par = (a, m, s.par_a) if w < 2 else (m, b, s.par_m)
                if u is None:
                    return
                steps, n = (qk_conv_steps, w * TAPS) if w < 2 else (v_conv_steps, 0)
                if 0 in which:
                    if w < 2:
                        wait(dve, qk_pre_ready, u, w + 1)
                    else:
                        wait(dve, v_pre_ready, u, 1)
                    if before is not None:
                        if w < 2:
                            wait(dve, squares_rest_ready, before, w + 1)
                        else:
                            wait(dve, v_silu_ready, before, 1)
                    nc.vector.tensor_scalar(conv[:, w], pre[:, w, :, 0:P], taps[par][:, w, 0:1], None,
                                            ALU.mult).then_inc(steps.sem, 1)
                for t in which:
                    if t == 0:
                        continue
                    wait(dve, steps, u, n + t)
                    nc.vector.scalar_tensor_tensor(conv[:, w], pre[:, w, :, t:t + P], taps[par][:, w, t:t + 1], conv[:, w],
                                                   ALU.mult, ALU.add).then_inc(steps.sem, 1)

            def scale(l):
                if m is None:
                    return
                wait(dve, level_done, m, l + 1)
                if l == 0:
                    wait(dve, unit_ready, m, 1)
                else:
                    wait(dve, scaled, m, l)
                blocks = UC >> (l + 1)
                pair = total[l][:].rearrange("p (m two) -> p m two", two=2)
                second_halves = halves(KQ[:], l, 1)
                nc.vector.tensor_tensor(second_halves, second_halves,
                                        pair[:, :, 0:1].unsqueeze(1).to_broadcast([P, 2, blocks, 1 << l]), ALU.mult)
                nc.vector.tensor_tensor(total[l + 1][:], pair[:, :, 0], pair[:, :, 1], ALU.mult).then_inc(scaled.sem, 1)

            def keep_diagonal():
                if m is None:
                    return
                wait_apart(dve, diag_done.sem, diag_done.at(m, 1), dve_waits_passed)
                if b is not None:
                    wait_apart(dve, pairs_kept.sem, pairs_kept.at(b, 1), dve_waits_passed)
                nc.vector.copy_predicated(by_batch(all_pairs[:, 1]), on_each_batch(ident[:].bitcast(I32)),
                                          by_batch(bank[4][:])).then_inc(pairs_ready.sem, 1)

            def keep_pairs(l):
                if m is None:
                    return
                src = bank[3 + l % 2][:].rearrange("p (k m s) -> p k m s", k=2, s=1 << l)
                mask = level_mask[:, l].rearrange("p (m s) -> p m s", s=1 << l)
                wait_apart(dve, pairs_ready.sem, pairs_ready.at(m, l + 1), dve_waits_passed)
                nc.vector.copy_predicated(halves(all_pairs[:], l, 1),
                                          mask.bitcast(I32).unsqueeze(1).to_broadcast([P, 2, UC >> (l + 1), 1 << l]), src)
                if b is not None:
                    if l == 0:
                        wait(dve, x1_ready, b, 1)
                        wait(dve, t1_ready, b, 1)
                    else:
                        wait(dve, z_done, b, l)
                nc.vector.scalar_tensor_tensor(halves(pairs[:, l], l, 1), src[:, 0], 1.0 / GRAIN, mask, ALU.mult,
                                               ALU.mult).then_inc(pairs_ready.sem, 1)

            def first_inverse():
                if m is None:
                    return
                wait(dve, t_done, m, 1)
                nc.vector.tensor_tensor(T_inv[:], bank[7][:], ident_each[:], ALU.add).then_inc(t1_ready.sem, 1)

            def add_identity_to_z(l):
                if b is None:
                    return
                wait(dve, z_done, b, l)
                nc.vector.tensor_tensor(halves(ZI[:, l - 1], l, 0),
                                        bank[5][:, 0:UC // 2].rearrange("p (m s) -> p m s", s=1 << l),
                                        halves(ident_each[:], l, 0), ALU.add).then_inc(zi_ready.sem, 1)

            def take_residual(n):
                if b is None:
                    return
                wait(dve, product_done, b, n + 1)
                if n == 0:
                    wait(dve, u_kept, b, 1)
                nc.vector.tensor_tensor(residual[:], bank[7][:], U_sb[:], ALU.add).then_inc(residual_ready.sem, 1)

            def correct_delta(n):
                if b is None:
                    return
                wait(dve, correction_done, b, n + 1)
                if n >= 1:
                    wait(dve, delta_refined, b, n)
                nc.vector.tensor_tensor(delta[:], delta[:], bank[5][:], ALU.add).then_inc(delta_refined.sem, 1)

            def unit_inputs():
                if a is None:
                    return
                wait(dve, rnorm_ready, a, 2)
                wait(dve, unit_loaded, a, 32)
                nc.vector.tensor_tensor(k_hat[:], silu[:, 1], rnorm[:, 1], ALU.mult)
                nc.vector.scalar_tensor_tensor(q_hat[:], silu[:, 0], SCALE, rnorm[:, 0], ALU.mult,
                                               ALU.mult).then_inc(hats_ready.sem, 1)
                wait(dve, hats_ready, a, 1)
                if m is not None:
                    wait(dve, k_transposed, m, 1)
                nc.vector.tensor_tensor(KR[:], k_hat[:], beta_u[:], ALU.mult)
                if m is not None:
                    wait(dve, scan_ready, m, 1)
                nc.vector.scalar_tensor_tensor(KQ[:, 0], k_hat[:], -1.0, decay_u[:], ALU.mult, ALU.mult)
                nc.vector.tensor_tensor(KQ[:, 1], q_hat[:], decay_u[:], ALU.mult).then_inc(unit_ready.sem, 1)

            halo(a, s.a_first, m, qk_conv_steps, 2 * TAPS, slice(0, 2), qk_halo_ready)
            halo(m, s.m_first, b, v_conv_steps, TAPS, slice(2, 3), v_halo_ready)
            add_identity_to_z(1)
            keep_diagonal()
            scale(0)
            keep_pairs(0)
            for l in range(1, LEVELS - 1):
                add_identity_to_z(l + 1)
                scale(l)
                keep_pairs(l)
                if l >= 2:
                    convolve(l // 2 - 1, range(l % 2 * 2, l % 2 * 2 + 2))
            convolve(2, range(2))
            take_residual(0)
            scale(LEVELS - 1)
            correct_delta(0)
            keep_pairs(LEVELS - 1)
            take_residual(1)
            correct_delta(1)
            convolve(2, range(2, TAPS))
            if b is not None:
                wait(dve, o_done, b, 1)
                wait(dve, gate_ready, b, 1)
                nc.vector.tensor_tensor(yg[:], bank[6][:], gate[:], ALU.mult).then_inc(yg_ready.sem, 1)
                wait(dve, s_done, b, 1)
                if s.ends:
                    nc.vector.memset(state[:], 0.0).then_inc(state_ready.sem, 1)
                else:
                    wait(dve, chunk_decay_ready, b, 1)
                    for i in range(B):
                        last = nc.vector.scalar_tensor_tensor(state[:, cols(i)], state[:, cols(i)], chunk_decay[:, i:i + 1],
                                                              bank[7][:, cols(i)], ALU.mult, ALU.add)
                    last.then_inc(state_ready.sem, 1)
            if m is not None:
                wait(dve, scaled, m, LEVELS)
                if b is not None:
                    dve.wait_ge(state_ready.sem, b + 2)
                nc.vector.tensor_copy(chunk_decay[:], total[LEVELS][:]).then_inc(chunk_decay_ready.sem, 1)
            unit_inputs()
            first_inverse()
            if b is not None:
                wait(dve, y_rn_ready, b, 1)
                dve.wait_ge(y_stored, b * 16 + 16)
                nc.vector.scalar_tensor_tensor(y_out[:], yg[:], norm_w_col[:, 0:1], y_rn[:], ALU.mult,
                                               ALU.mult).then_inc(y_ready.sem, 1)

        walk(dve, step)

    @block.scalar
    def _(act):
        act.sem_inc(y_stored, 16)
        act.sem_inc(y_sums_free, 1)

        def step(s):
            a, m, b = s.a, s.m, s.b

            def take_projection(w):
                u = a if w < 2 else m
                if u is None:
                    return
                projected, halo_ready, ready, n = (qk_projected, qk_halo_ready, qk_pre_ready, w + 1) if w < 2 else \
                    (v_projected, v_halo_ready, v_pre_ready, 1)
                wait(act, projected, u, n)
                if w != 1:
                    wait(act, halo_ready, u, 1)
                nc.scalar.activation(pre[:, w, :, HALO:HALO + P], by_batch(bank[w % 2][:]),
                                     ACT.Copy).then_inc(ready.sem, 1)

            def silu_squares(w):
                if a is None:
                    return
                wait(act, qk_conv_steps, a, (w + 1) * TAPS)
                if w == 0 and m is not None:
                    wait(act, unit_ready, m, 1)
                nc.scalar.activation(silu[:, w], conv[:, w].rearrange("p b t -> p (b t)"),
                                     ACT.Silu).then_inc(silu_ready.sem, 1)
                wait(act, silu_ready, a, w + 1)
                nc.scalar.activation(squares[:, w], silu[:, w], ACT.Square).then_inc(squares_ready.sem, 1)

            def silu_v():
                if b is None:
                    return
                wait(act, v_conv_steps, b, TAPS)
                nc.scalar.activation(v_u[:], conv[:, 2].rearrange("p b t -> p (b t)"),
                                     ACT.Silu).then_inc(v_silu_ready.sem, 1)

            def silu_gate():
                if b is None:
                    return
                wait(act, gate_projected, b, 1)
                nc.scalar.activation(gate[:], bank[1][:], ACT.Silu, bias=bg_col[s.par_b][:, 0:1]).then_inc(gate_ready.sem, 1)

            def inverse_norm(w):
                if a is None:
                    return
                wait(act, sums_done, a, w + 1)
                if w == 0 and m is not None:
                    wait(act, unit_ready, m, 1)
                nc.scalar.activation(rnorm[:, w], bank[2][:], ACT.Ln, bias=l2_eps[:, 0:1]).then_inc(sums_taken.sem, 1)
                wait(act, sums_taken, a, w + 1)
                nc.scalar.activation(rnorm[:, w], rnorm[:, w], ACT.Exp, scale=-0.5).then_inc(rnorm_ready.sem, 1)

            def take_t(l):
                if b is None:
                    return
                wait(act, t_done, b, l + 1)
                nc.scalar.activation(halves(T_inv[:], l, 0), bank[7][:, 0:UC // 2].rearrange("p (m s) -> p m s", s=1 << l),
                                     ACT.Copy).then_inc(t_ready.sem, 1)

            def take_x(l):
                if b is None:
                    return
                wait(act, x_done, b, l)
                nc.scalar.activation(halves(X[:], l, 1), bank[6][:, 0:UC // 2].rearrange("p (m s) -> p m s", s=1 << l),
                                     ACT.Copy).then_inc(x_ready.sem, 1)

            silu_gate()
            take_projection(0)
            take_t(1)
            take_x(1)
            silu_v()
            take_t(2)
            take_x(2)
            take_projection(1)
            take_t(3)
            take_x(3)
            take_t(4)
            take_x(4)
            silu_squares(0)
            take_t(5)
            take_x(5)
            if b is not None:
                wait(act, u_done, b, 1)
                nc.scalar.activation(U_r[:], bank[7][:], ACT.Copy).then_inc(u_ready.sem, 1)
                nc.scalar.activation(U_sb[:], bank[7][:], ACT.Copy).then_inc(u_kept.sem, 1)
            take_x(6)
            take_projection(2)
            if b is not None:
                wait(act, delta_done, b, 1)
                nc.scalar.activation(delta[:], bank[5][:], ACT.Copy).then_inc(delta_ready.sem, 1)
            silu_squares(1)
            nc.scalar.preload_act_table_set("natural_log_exp_and_others")
            inverse_norm(0)
            inverse_norm(1)
            if m is not None:
                wait(act, scaled, m, LEVELS)
                if b is not None:
                    wait(act, o_state_done, b, 1)
                nc.scalar.activation(KQ_scan[:], KQ[:], ACT.Copy).then_inc(scan_ready.sem, 1)
            if b is not None:
                wait(act, yg_ready, b, 1)
                nc.scalar.activation(y_sq[:], yg[:], ACT.Square).then_inc(y_sq_ready.sem, 1)
            if m is not None:
                wait(act, k_transposed, m, 1)
                if b is not None:
                    wait(act, s_done, b, 1)
                nc.scalar.activation(k_rows[:], bank[4][:], ACT.Copy).then_inc(k_rows_ready.sem, 1)
                wait(act, pairs_ready, m, LEVELS + 1)
                if b is not None:
                    wait(act, o_done, b, 1)
                nc.scalar.activation(pairs_scan[:], all_pairs[:], ACT.Copy).then_inc(pairs_kept.sem, 1)
            if b is not None:
                wait(act, y_sums_done, b, 1)
                nc.scalar.activation(y_rn[:], bank[2][:], ACT.Ln, bias=ln_eps[:, 0:1]).then_inc(y_sums_free, 1)
                act.wait_ge(y_sums_free, b + 2)
                nc.scalar.activation(y_rn[:], y_rn[:], ACT.Exp, scale=-0.5).then_inc(y_rn_ready.sem, 1)
                wait(act, y_ready, b, 1)
                act.dma_start(y_scratch[bass.ds(s.j, 1), :, :, bass.ds(s.h, 1), :].rearrange("a b v h t -> v (a b h) t"),
                              by_batch(y_out[:])).then_inc(y_stored, 16)

        walk(act, step)
        act.wait_ge(y_stored, 16 * (H * J + 1))

    @block.gpsimd
    def _(pool):
        def scale_keys(u, l):
            if l == 0:
                wait_apart(pool, unit_ready.sem, unit_ready.at(u, 1), pool_waits_passed)
            else:
                wait_apart(pool, scaled.sem, scaled.at(u, l), pool_waits_passed)
                wait_apart(pool, keys_scaled.sem, keys_scaled.at(u, l), pool_waits_passed)
            wait_apart(pool, level_done.sem, level_done.at(u, l + 1), pool_waits_passed)
            first_halves = halves(KR[:], l, 0)
            second = total[l][:].rearrange("p (m two) -> p m two", two=2)[:, :, 1:2]
            nc.gpsimd.tensor_tensor(first_halves, first_halves, second.to_broadcast([P, UC >> (l + 1), 1 << l]),
                                    ALU.mult).then_inc(keys_scaled.sem, 1)

        def squares_left(u, w):
            if u is None:
                return
            wait_apart(pool, silu_ready.sem, silu_ready.at(u, w + 1), pool_waits_passed)
            nc.gpsimd.tensor_tensor(conv[:, w].rearrange("p b t -> p (b t)"), silu[:, w], silu[:, w],
                                    ALU.mult).then_inc(square_ready.sem, 1)
            wait_apart(pool, square_ready.sem, square_ready.at(u, w + 1), pool_waits_passed)
            wait_apart(pool, squares_ready.sem, squares_ready.at(u, w + 1), pool_waits_passed)
            nc.gpsimd.tensor_tensor(squares_rest[:, w], conv[:, w].rearrange("p b t -> p (b t)"), squares[:, w],
                                    ALU.subtract).then_inc(squares_rest_ready.sem, 1)

        def step(s):
            if s.m is None:
                squares_left(s.a, 0)
                squares_left(s.a, 1)
                return
            for l in range(LEVELS):
                if l >= LEVELS - 2:
                    squares_left(s.a, l - (LEVELS - 2))
                scale_keys(s.m, l)
            wait_apart(pool, t_done.sem, t_done.at(s.m, 1), pool_waits_passed)
            nc.gpsimd.tensor_tensor(X[:], pairs[:, 0], ident_each[:], ALU.add).then_inc(x1_ready.sem, 1)

        walk(pool, step)


def mixture(nc, ctx, env):
    (x, Wo, gate_W, W1, b1, W2, b2, out, y_scratch, bank, ident, ones, ln_eps) = (env[n] for n in (
        "x", "Wo", "gate_W", "W1", "b1", "W2", "b2", "out", "y_scratch", "bank", "ident", "ones", "ln_eps"))
    (B, T, D, H, KC, J, E, FF, FCH, NF, LN_EPS) = (env[n] for n in (
        "B", "T", "D", "H", "KC", "J", "E", "FF", "FCH", "NF", "LN_EPS"))
    TOP = 2
    HALF_T = T // 2
    HALVES = T // 512
    GROUPS = HALVES * TOP * NF
    LAST = FCH[-1][1]

    def sb(name, shape, dt=F32):
        return ctx.enter_context(nc.sbuf_tensor(name, shape, dt))

    def sem(name):
        return ctx.enter_context(nc.semaphore(name))

    wo = sb("wo", [P, H, D])
    gate_w = sb("gate_w", [P, KC, E])
    y_in = [sb(f"y_in{p}", [P, H, P]) for p in range(2)]
    x_in = [sb(f"x_in{p}", [P, D]) for p in range(2)]
    x1 = sb("x1", [P, J, D])
    xn = [sb(f"xn{p}", [P, D]) for p in range(2)]
    xnT = sb("xnT", [P, KC, T])
    stats = sb("stats2", [P, 6])
    mv = sb("mv2", [P, 2])
    log_var = sb("log_var2", [P, 1])
    rstd = sb("rstd2", [P, 1])
    token_sum = sb("token_sum", [P, KC])
    logits = sb("logits", [1, 8])
    top_val = sb("top_val", [1, 8])
    top_idx = sb("top_idx", [1, 8], U32)
    neg_max = sb("neg_max", [1, 1])
    exps = sb("exps", [1, E])
    exp_sum = sb("exp_sum", [1, 1])
    top_exp = sb("top_exp", [1, TOP])
    inv_sum = sb("inv_sum", [1, 1])
    top_prob = sb("top_prob", [1, TOP])
    prob_sum = sb("prob_sum", [1, 1])
    inv_prob = sb("inv_prob", [1, 1])
    share = sb("share", [1, TOP])
    share_all = sb("share_all", [P, TOP])
    w1 = sb("w1", [P, TOP, KC, FF])
    b1_col = sb("b1_col", [P, TOP, NF])
    w2 = sb("w2", [P, TOP, NF, D])
    w2_share = sb("w2_share", [P, TOP, NF, D])
    b2_row = sb("b2_row", [1, TOP, D])
    b2_part = sb("b2_part", [1, D])
    b2_mix = sb("b2_mix", [1, D])
    hT = sb("hT", [P, TOP, NF, T])
    o_out = [sb(f"o_out{p}", [P, D]) for p in range(2)]

    consts_loaded = sem("consts_loaded2")
    tile_loaded = [sem(f"tile_loaded{p}") for p in range(2)]
    first_loaded = [sem(f"first_loaded{n}") for n in range(TOP)]
    experts_loaded = sem("experts_loaded")
    out_stored = [sem(f"out_stored{p}") for p in range(2)]
    attn_done = sem("attn_done")
    x1_ready = sem("x1_ready")
    ln_steps = sem("ln_steps2")
    xn_ready = sem("xn_ready2")
    xn_transposed = sem("xn_transposed")
    xnT_ready = sem("xnT_ready")
    token_sum_ready = sem("token_sum_ready")
    logits_done = sem("logits_done")
    route_steps = sem("route_steps")
    pads_ready = sem("pads_ready")
    dve_waits_passed, sp_waits_passed = sem("dve_waits_passed2"), sem("sp_waits_passed")
    choice_ready = sem("choice_ready")
    exps_ready = sem("exps_ready")
    share_ready = sem("share_ready")
    share_spread = sem("share_spread")
    mix_steps = sem("mix_steps")
    w2_ready = sem("w2_ready")
    h_done = sem("h_done")
    h_ready = sem("h_ready")
    ffn_done = sem("ffn_done")
    o_ready = sem("o_ready")
    EXPERT_LOADS = 16 * TOP * 3
    FIRST_LOADS = 16 * 3
    ROUTE_STEPS = 7

    block = ctx.enter_context(nc.Block())

    @block.sync
    def _(sp):
        sp.dma_start(wo[:], Wo.rearrange("(h v) d -> v h d", v=P)).then_inc(consts_loaded, 16)
        for k in range(KC):
            sp.dma_start(gate_w[:, k, :], gate_W.rearrange("e (k p) -> p k e", p=P)[:, k, :],
                         allow_slow_non_contiguous=True).then_inc(consts_loaded, 16)
        with sp.Fori(0, B) as b:
            for j in range(J):
                sp.wait_ge(x1_ready, b * J + (j + 1))
                sp.dma_start(y_in[j % 2][:], y_scratch[j, bass.ds(b, 1)].rearrange("a v h t -> (a v) h t")) \
                    .then_inc(tile_loaded[j % 2], 16)
                sp.dma_start(x_in[j % 2][:], x[bass.ds(b, 1), j * P:(j + 1) * P, :].rearrange("a t d -> (a t) d")) \
                    .then_inc(tile_loaded[j % 2], 16)
            wait_apart(sp, choice_ready, b + 1, sp_waits_passed)
            chosen = [sp.value_load(top_idx[0:1, n:n + 1], min_val=0, max_val=E - 1) for n in range(TOP)]
            for n, e in enumerate(chosen):
                at = bass.ds(e, 1)
                sp.dma_start(w1[:, n], W1[at].rearrange("a (k p) f -> p (a k) f", p=P)).then_inc(first_loaded[n], 16)
                sp.dma_start(b1_col[:, n, 0:2], b1[at, 0:256].rearrange("a (c p) -> p (a c)", p=P),
                             allow_slow_non_contiguous=True).then_inc(first_loaded[n], 16)
                sp.dma_start(b1_col[0:LAST, n, 2:3], b1[at, 256:FF].rearrange("a p -> p a"),
                             allow_slow_non_contiguous=True).then_inc(first_loaded[n], 16)
            for n, e in enumerate(chosen):
                at = bass.ds(e, 1)
                sp.dma_start(w2[:, n, 0:2], W2[at, 0:256, :].rearrange("a (c p) d -> p (a c) d", p=P)).then_inc(experts_loaded, 16)
                sp.dma_start(w2[0:LAST, n, 2], W2[at, 256:FF, :].rearrange("a p d -> (a p) d")).then_inc(experts_loaded, 16)
                sp.dma_start(b2_row[:, n], b2[at, :]).then_inc(experts_loaded, 16)

    @block.tensor
    def _(pe):
        def transpose_tile(b, j):
            pe.wait_ge(xn_ready, b * J + (j + 1))
            if j >= 2:
                pe.wait_ge(xnT_ready, b * J + (j - 1))
            for k in range(KC):
                last = nc.tensor.transpose(bank[2 + j % 2][:, k * P:(k + 1) * P], xn[j % 2][:, k * P:(k + 1) * P], ident[:])
            last.then_inc(xn_transposed, 1)

        pe.wait_ge(consts_loaded, 16 * (1 + KC))
        with pe.Fori(0, B) as b:
            for j in range(J):
                pe.wait_ge(tile_loaded[j % 2], b * (16 * J) + 32 * (j // 2 + 1))
                for h in range(H):
                    last = nc.tensor.matmul(bank[j % 2][:], y_in[j % 2][:, h, :], wo[:, h, :], start=h == 0, stop=h == H - 1)
                last.then_inc(attn_done, 1)
                if j >= 1:
                    transpose_tile(b, j - 1)
            transpose_tile(b, J - 1)
            pe.wait_ge(token_sum_ready, b + 1)
            for k in range(KC):
                last = nc.tensor.matmul(bank[2][0:1, 0:E], token_sum[:, k:k + 1], gate_w[:, k, :], start=k == 0, stop=k == KC - 1)
            last.then_inc(logits_done, 1)
            pe.wait_ge(share_ready, b + 1)
            nc.tensor.matmul(bank[3][:, 0:TOP], ones[0:1, :], share[:], start=True, stop=True).then_inc(share_spread, 1)
            g = 0
            for t in range(HALVES):
                for n in range(TOP):
                    if t == 0:
                        pe.wait_ge(first_loaded[n], b * FIRST_LOADS + FIRST_LOADS)
                    for c, (f0, fn) in enumerate(FCH):
                        if g >= 2:
                            pe.wait_ge(h_ready, b * GROUPS + (g - 1))
                        for k in range(KC):
                            last = nc.tensor.matmul(bank[4 + g % 2][0:fn, :], w1[:, n, k, f0:f0 + fn],
                                                    xnT[:, k, t * 512:(t + 1) * 512], start=k == 0, stop=k == KC - 1)
                        last.then_inc(h_done, 1)
                        g += 1
            pe.wait_ge(w2_ready, b + 1)
            pe.wait_ge(h_ready, b * GROUPS + GROUPS)
            for j in range(J):
                if j >= 2:
                    pe.wait_ge(o_ready, b * J + (j - 1))
                to = bank[6 + j % 2]
                nc.tensor.matmul(to[:], ones[0:1, :], b2_mix[:], start=True, stop=False)
                for n in range(TOP):
                    for c, (f0, fn) in enumerate(FCH):
                        last = nc.tensor.matmul(to[:], hT[0:fn, n, c, j * P:(j + 1) * P], w2_share[0:fn, n, c], start=False,
                                                stop=n == TOP - 1 and c == NF - 1)
                last.then_inc(ffn_done, 1)

    @block.vector
    def _(dve):
        nc.vector.memset(logits[:], -3.0e38).then_inc(pads_ready, 1)
        dve.sem_inc(x1_ready, 2)
        dve.wait_ge(pads_ready, 1)
        with dve.Fori(0, B) as b:
            for j in range(J):
                p = j % 2
                n = b * J + j
                dve.wait_ge(attn_done, b * J + (j + 1))
                dve.wait_ge(tile_loaded[p], b * (16 * J) + 32 * (j // 2 + 1))
                nc.vector.tensor_tensor(x1[:, j], bank[p][:], x_in[p][:], ALU.add).then_inc(x1_ready, 1)
                dve.wait_ge(x1_ready, b * J + (j + 3))
                nc.vector.bn_stats(stats[:], x1[:, j]).then_inc(ln_steps, 1)
                wait_apart(dve, ln_steps, b * (4 * J) + (4 * j + 1), dve_waits_passed)
                nc.vector.bn_aggr(mv[:], stats[:]).then_inc(ln_steps, 1)
                dve.wait_ge(ln_steps, b * (4 * J) + (4 * j + 4))
                if j >= 2:
                    dve.wait_ge(xn_transposed, b * J + (j - 1))
                nc.vector.tensor_scalar(xn[p][:], x1[:, j], mv[:, 0:1], rstd[:], ALU.subtract, ALU.mult).then_inc(xn_ready, 1)
            dve.wait_ge(xnT_ready, b * J + J)
            nc.vector.tensor_reduce(token_sum[:], xnT[:], AX_X, ALU.add).then_inc(token_sum_ready, 1)
            R = ROUTE_STEPS
            steps = [0]

            def chained(ins):
                ins.then_inc(route_steps, 1)
                steps[0] += 1
                wait_apart(dve, route_steps, b * R + steps[0], dve_waits_passed)

            dve.wait_ge(logits_done, b + 1)
            chained(nc.vector.tensor_scalar(logits[:, 0:E], bank[2][0:1, 0:E], 1.0 / T, None, ALU.mult))
            chained(nc.vector.max(top_val[:], logits[:]))
            nc.vector.max_index(top_idx[:], top_val[:], logits[:]).then_inc(choice_ready, 1)
            chained(nc.vector.tensor_scalar(neg_max[:], top_val[:, 0:1], -1.0, None, ALU.mult))
            dve.wait_ge(exps_ready, b * 2 + 2)
            chained(nc.vector.reciprocal(inv_sum[:], exp_sum[:]))
            chained(nc.vector.tensor_scalar(top_prob[:], top_exp[:], inv_sum[:], None, ALU.mult))
            chained(nc.vector.tensor_tensor(prob_sum[:], top_prob[:, 0:1], top_prob[:, 1:2], ALU.add))
            chained(nc.vector.reciprocal(inv_prob[:], prob_sum[:]))
            nc.vector.tensor_scalar(share[:], top_prob[:], inv_prob[:], None, ALU.mult).then_inc(share_ready, 1)
            dve.wait_ge(share_spread, b + 1)
            nc.vector.tensor_copy(share_all[:], bank[3][:, 0:TOP]).then_inc(mix_steps, 1)
            dve.wait_ge(experts_loaded, b * EXPERT_LOADS + EXPERT_LOADS)
            dve.wait_ge(mix_steps, b * 2 + 1)
            dve.wait_ge(share_ready, b + 1)
            nc.vector.tensor_scalar(b2_part[:], b2_row[:, 0], share[:, 0:1], None, ALU.mult).then_inc(mix_steps, 1)
            for n in range(TOP):
                nc.vector.tensor_scalar(w2_share[:, n, 0:2], w2[:, n, 0:2], share_all[:, n:n + 1], None, ALU.mult)
                nc.vector.tensor_scalar(w2_share[0:LAST, n, 2], w2[0:LAST, n, 2], share_all[0:LAST, n:n + 1], None, ALU.mult)
            dve.wait_ge(mix_steps, b * 2 + 2)
            nc.vector.scalar_tensor_tensor(b2_mix[:], b2_row[:, 1], share[:, 1:2], b2_part[:], ALU.mult,
                                           ALU.add).then_inc(w2_ready, 1)
            for j in range(J):
                dve.wait_ge(ffn_done, b * J + (j + 1))
                dve.wait_ge(out_stored[j % 2], b * (8 * J) + 16 * (j // 2 + 1))
                nc.vector.tensor_tensor(o_out[j % 2][:], bank[6 + j % 2][:], x1[:, j], ALU.add).then_inc(o_ready, 1)

    @block.scalar
    def _(act):
        for p in range(2):
            act.sem_inc(out_stored[p], 16)
        with act.Fori(0, B) as b:
            nc.scalar.preload_act_table_set("natural_log_exp_and_others")
            for j in range(J):
                act.wait_ge(ln_steps, b * (4 * J) + (4 * j + 2))
                nc.scalar.activation(log_var[:], mv[:, 1:2], ACT.Ln, bias=ln_eps[:, 0:1]).then_inc(ln_steps, 1)
                act.wait_ge(ln_steps, b * (4 * J) + (4 * j + 3))
                nc.scalar.activation(rstd[:], log_var[:], ACT.Exp, scale=-0.5).then_inc(ln_steps, 1)
                act.wait_ge(xn_transposed, b * J + (j + 1))
                nc.scalar.activation(xnT[:, :, j * P:(j + 1) * P], bank[2 + j % 2][:].rearrange("p (k t) -> p k t", k=KC),
                                     ACT.Copy).then_inc(xnT_ready, 1)
            act.wait_ge(route_steps, b * ROUTE_STEPS + 3)
            nc.scalar.activation(exps[:], logits[:, 0:E], ACT.Exp, bias=neg_max[:], accum_out=exp_sum[:]).then_inc(exps_ready, 1)
            nc.scalar.activation(top_exp[:], top_val[:, 0:TOP], ACT.Exp, bias=neg_max[:]).then_inc(exps_ready, 1)
            g = 0
            for t in range(HALVES):
                for n in range(TOP):
                    for c, (f0, fn) in enumerate(FCH):
                        act.wait_ge(h_done, b * GROUPS + (g + 1))
                        nc.scalar.activation(hT[0:fn, n, c, t * 512:(t + 1) * 512], bank[4 + g % 2][0:fn, :], ACT.Gelu,
                                             bias=b1_col[0:fn, n, c:c + 1]).then_inc(h_ready, 1)
                        g += 1
            for j in range(J):
                act.wait_ge(o_ready, b * J + (j + 1))
                act.dma_start(out[bass.ds(b, 1), j * P:(j + 1) * P, :].rearrange("a t d -> (a t) d"),
                              o_out[j % 2][:]).then_inc(out_stored[j % 2], 16)
        for p in range(2):
            act.wait_ge(out_stored[p], 16 + 16 * (B * J // 2))


_INS = ["hidden_states", "Wq", "Wk", "Wv", "conv_q", "conv_k", "conv_v", "Wf1", "Wf2", "Wb", "A_log", "dt_bias", "Wg",
        "bg", "norm_w", "Wo"]
_INS = ["L0_attn_" + n for n in _INS] + ["L0_ffn_" + n for n in ("gate_W", "W1", "b1", "W2", "b2")]


def kernel(**inputs):
    import numpy as _np
    import concourse.bacc as _bacc
    from concourse import mybir as _mybir
    from concourse.bass_utils import run_bass_kernel_spmd as _run

    nc = _bacc.Bacc("TRN2", target_bir_lowering=False, num_devices=1)
    arrays, args = {}, []
    for name in _INS:
        a = _np.ascontiguousarray(inputs[name])
        arrays[f"in_{name}"] = a
        args.append(nc.dram_tensor(f"in_{name}", a.shape, _mybir.dt.from_np(a.dtype), kind="ExternalInput").ap())
    shape = inputs["L0_attn_hidden_states"].shape
    args.append(nc.dram_tensor("out_0", shape, _mybir.dt.from_np(_np.dtype("float32")), kind="ExternalOutput").ap())
    preln_delta_moe(nc, *args)
    r = _run(nc, [arrays], core_ids=[0])
    return r.results[0]["out_0"]
```
